# Optimizing a Trainium2 kernel written in Bass

```python
import numpy as np
import jax
import jax.numpy as jnp

def _softmax(x, axis=-1):
    return jax.nn.softmax(x, axis=axis)

def _gelu(x):
    return jax.nn.gelu(x, approximate=True)

def _silu(x):
    return jax.nn.silu(x)

def _sigmoid(x):
    return jax.nn.sigmoid(x)

def _layernorm(x, axis=-1, eps=1e-05):
    m = jnp.mean(x, axis=axis, keepdims=True)
    v = jnp.var(x, axis=axis, keepdims=True)
    return (x - m) / jnp.sqrt(v + eps)

def _scatter_add(tgt, idx, src, axis=0):
    return tgt.at[idx].add(src)

def _segment_sum(src, seg, n):
    return jax.ops.segment_sum(src, seg, n)
kernel_name = 'mk_adaln_d1_jaxref_r8_d071d9'

def setup_inputs(seed: int=0):
    np.random.seed(seed)
    _w = jnp.asarray

    def _L0_attn_setup():
        import jax, jax.numpy as jnp
        import numpy as np
        BLOCK_H = 32
        BLOCK_W = 32
        N_FEAT = 512
        K_FEAT = 512
        key = jax.random.key(seed)
        k1, k2, k3 = jax.random.split(key, 3)
        data = jax.random.normal(k1, (4, 128, K_FEAT), dtype=jnp.float32)
        weight = jax.random.normal(k2, (N_FEAT, K_FEAT), dtype=jnp.float32) * 0.02
        nb, kb = (N_FEAT // BLOCK_H, K_FEAT // BLOCK_W)
        block_pattern = jax.random.randint(k3, (nb, kb), 0, 2, dtype=jnp.int32)
        mask = jnp.repeat(jnp.repeat(block_pattern, BLOCK_H, axis=0), BLOCK_W, axis=1)
        return {'data': data, 'weight': weight, 'mask': mask}
    _L0_attn_in = _L0_attn_setup()

    def _L0_ffn_setup():
        import jax, jax.numpy as jnp
        import numpy as np
        HIDDEN = 512
        INTER = 1376
        SPARSITY = 0.5

        def _ternary_weight(key, out_dim, in_dim, sparsity):
            k_mask, k_sign = jax.random.split(key)
            nonzero = jax.random.bernoulli(k_mask, 1.0 - sparsity, (out_dim, in_dim))
            sign = jnp.where(jax.random.bernoulli(k_sign, 0.5, (out_dim, in_dim)), 1.0, -1.0)
            return (nonzero * sign).astype(jnp.float32)
        key = jax.random.key(seed)
        kx, kg, ku, kd, ksg, ksu, ksd = jax.random.split(key, 7)
        x = jax.random.normal(kx, (4, 256, HIDDEN), dtype=jnp.float32)
        Wg = _ternary_weight(kg, INTER, HIDDEN, SPARSITY)
        Wu = _ternary_weight(ku, INTER, HIDDEN, SPARSITY)
        Wd = _ternary_weight(kd, HIDDEN, INTER, SPARSITY)
        ag = jax.random.uniform(ksg, (INTER,), dtype=jnp.float32, minval=0.5, maxval=1.5) / np.sqrt(HIDDEN)
        au = jax.random.uniform(ksu, (INTER,), dtype=jnp.float32, minval=0.5, maxval=1.5) / np.sqrt(HIDDEN)
        ad = jax.random.uniform(ksd, (HIDDEN,), dtype=jnp.float32, minval=0.5, maxval=1.5) / np.sqrt(INTER)
        return {'x': x, 'Wg': Wg, 'Wu': Wu, 'Wd': Wd, 'ag': ag, 'au': au, 'ad': ad}
    _L0_ffn_in = _L0_ffn_setup()
    _L0_c = _w((lambda *s: np.random.randn(*s).astype(np.float32) * 0.05)(2, 512))
    _L0_wmod = _w((lambda *s: np.random.randn(*s).astype(np.float32) * 0.05)(512, 6 * 512) * 512 ** (-0.5))
    _d = {'L0_attn_data': _L0_attn_in['data'], 'L0_attn_weight': _L0_attn_in['weight'], 'L0_attn_mask': _L0_attn_in['mask'], 'L0_ffn_Wg': _L0_ffn_in['Wg'], 'L0_ffn_Wu': _L0_ffn_in['Wu'], 'L0_ffn_Wd': _L0_ffn_in['Wd'], 'L0_ffn_ag': _L0_ffn_in['ag'], 'L0_ffn_au': _L0_ffn_in['au'], 'L0_ffn_ad': _L0_ffn_in['ad'], 'L0_c': _L0_c, 'L0_wmod': _L0_wmod}
    _x0 = _d['L0_attn_data']
    _d['L0_attn_data'] = jax.random.normal(jax.random.fold_in(jax.random.key(seed), 1), (2, 512, 512), dtype=_x0.dtype)
    del _x0
    return _d

def reference(L0_attn_data, L0_attn_weight, L0_attn_mask, L0_ffn_Wg, L0_ffn_Wu, L0_ffn_Wd, L0_ffn_ag, L0_ffn_au, L0_ffn_ad, L0_c, L0_wmod):

    def _L0_attn_ref(data, weight, mask):
        import jax, jax.numpy as jnp
        import numpy as np
        BLOCK_H = 32
        BLOCK_W = 32
        N_FEAT = 512
        K_FEAT = 512
        N, K = weight.shape
        nb, kb = (N // BLOCK_H, K // BLOCK_W)
        block_mask = mask.reshape(nb, BLOCK_H, kb, BLOCK_W).astype(jnp.float32).sum(axis=(1, 3)) > 0
        elem_mask = jnp.repeat(jnp.repeat(block_mask, BLOCK_H, axis=0), BLOCK_W, axis=1)
        w_masked = weight * elem_mask.astype(weight.dtype)
        out = jnp.einsum('bsk,nk->bsn', data, w_masked)
        return out

    def _L0_ffn_ref(x, Wg, Wu, Wd, ag, au, ad):
        import jax, jax.numpy as jnp
        import numpy as np
        HIDDEN = 512
        INTER = 1376
        SPARSITY = 0.5

        def _ternary_weight(key, out_dim, in_dim, sparsity):
            k_mask, k_sign = jax.random.split(key)
            nonzero = jax.random.bernoulli(k_mask, 1.0 - sparsity, (out_dim, in_dim))
            sign = jnp.where(jax.random.bernoulli(k_sign, 0.5, (out_dim, in_dim)), 1.0, -1.0)
            return (nonzero * sign).astype(jnp.float32)
        gate = jnp.einsum('bsh,ih->bsi', x, Wg) * ag
        up = jnp.einsum('bsh,ih->bsi', x, Wu) * au
        h = jax.nn.silu(gate) * up
        out = jnp.einsum('bsi,hi->bsh', h, Wd) * ad
        return out
    x = L0_attn_data
    mod = (_silu(L0_c) @ L0_wmod).reshape(L0_c.shape[0], 6, 1, -1)
    sa, ca, ga, sb, cb, gb = (mod[:, 0], mod[:, 1], mod[:, 2], mod[:, 3], mod[:, 4], mod[:, 5])
    ga = (2 * (ga >= 0) - 1) * jnp.maximum(jnp.abs(ga), 0.25)
    gb = (2 * (gb >= 0) - 1) * jnp.maximum(jnp.abs(gb), 0.25)
    h = _layernorm(x, axis=-1) * (1 + ca) + sa
    x = x + ga * _L0_attn_ref(h, L0_attn_weight, L0_attn_mask)
    h = _layernorm(x, axis=-1) * (1 + cb) + sb
    x = x + gb * _L0_ffn_ref(h, L0_ffn_Wg, L0_ffn_Wu, L0_ffn_Wd, L0_ffn_ag, L0_ffn_au, L0_ffn_ad)
    return x

_drawn_inputs = setup_inputs


def setup_inputs(seed=0):
    import zlib

    import numpy as np

    out = dict(_drawn_inputs(seed))
    spreads = {}
    factors = {'L0_ffn_ag': 3.044, 'L0_ffn_au': 3.55, 'L0_ffn_ad': 3.581}
    for name, (base, spread) in spreads.items():
        noise = np.random.default_rng([zlib.crc32(name.encode()), seed]).standard_normal(out[name].shape)
        drawn = base * np.exp(spread * noise) if base else spread * noise
        out[name] = jnp.asarray(drawn.astype(out[name].dtype))
    for name, factor in factors.items():
        out[name] = (out[name] * factor).astype(out[name].dtype)
    return out
```

```python
from contextlib import ExitStack

import concourse.bass as bass
from concourse import mybir

F32 = mybir.dt.float32
F32R = mybir.dt.float32r
I32 = mybir.dt.int32
U16 = mybir.dt.uint16
U8 = mybir.dt.uint8
ALU = mybir.AluOpType
ACT = mybir.ActivationFunctionType
AX_X = mybir.AxisListType.X

P = 128
D = 512
KT = D // P
NB = 2
TT = 4
SEQ = TT * P
F = 1376
C = -(-F // P)
FT = F - (C - 1) * P
BLK = 32
NBLK = D // BLK
EPS = 1e-5
GATE_MIN = 0.25
STEPS = NB * C
LAG = 2
CHECKS_AT = {0: 1, 1: 2, 2: 2, 3: 2, 4: 1}
GROUPS = [(0, 3), (3, 6), (6, C)]
GROUP_OF = [g for g, (a, b) in enumerate(GROUPS) for _ in range(a, b)]


def gu_bank(s, u):
    return (2 * s + u + 2) % 3


def adaln_block(nc, x, att_w, att_mask, cond, mod_ln1, mod_ln2, mod_gate, w_gu, w_gu_tail, w_down,
                scales, scales_tail, down_scale, out):
    with ExitStack() as ctx:
        def sb(name, shape, dt=F32):
            return ctx.enter_context(nc.sbuf_tensor(name, shape, dt))

        def sem(name):
            return ctx.enter_context(nc.semaphore(name))

        xt = sb("xt", [P, NB * TT, D])
        xn = sb("xn", [P, TT, D])
        ht = sb("ht", [P, NB, KT, 2, SEQ], F32R)
        hbuf = sb("hbuf", [P, 2, SEQ])
        awork = sb("awork", [P, KT, D])
        maskt = sb("maskt", [P, KT, D], I32)
        wsplit = sb("wsplit", [P, KT * 2, D], F32R)
        modw = sb("modw", [P, 3, KT, D])
        rows = sb("rows", [P, 3, D])
        wffn = sb("wffn", [P, C, 3 * D])
        whi_gu = sb("whi_gu", [P, 2, 2 * D], F32R)
        whi_d2 = sb("whi_d2", [P, D], F32R)
        gscr = sb("gscr", [P, D])
        junk = sb("junk", [P, 3 * D], U8)
        scal = sb("scal", [P, C, 2])
        adb = sb("adb", [P, D])
        condt = sb("condt", [P, KT, NB])
        sc = sb("sc", [P, KT, BLK])
        ident = sb("ident", [P, P])
        blkones = sb("blkones", [P, P])
        sel = sb("sel", [P, NB])
        selb = sb("selb", [P, NB, P])
        oneplus = sb("oneplus", [P, 8])
        onecol = sb("onecol", [P, 1])
        msum = sb("msum", [P, KT, NBLK])
        keep = sb("keep", [P, KT, NBLK])
        modc = sb("modc", [P, 2, KT, 4])
        bns = sb("bns", [P, 2 * NB, TT, 6])
        mv = sb("mv", [P, 2 * NB, TT, 2])
        veps = sb("veps", [P, 2 * NB, TT])
        rstd = sb("rstd", [P, 2 * NB, TT])
        mhalf = sb("mhalf", [P, TT])
        chk = sb("chk", [P, C])
        flagv = sb("flagv", [P, len(GROUPS)])
        flags = sb("flags", [1, len(GROUPS)], I32)

        gates = maskt[:, :, :].bitcast(F32)
        silu_g = awork[:, 0:2, :]
        inner = awork[:, 2:4, :]

        def raw_gu(c, u, k):
            return wffn[:, c, (u * KT + k) * P:(u * KT + k + 1) * P]

        def raw_d(c):
            return wffn[:, c, 2 * D:3 * D]

        def whi_d(s):
            return wsplit[:, 6 + s % 3, :] if s % 3 < 2 else whi_d2[:, :]

        bank = [ctx.enter_context(nc.psum_tensor(f"bank{i}", [P, D], F32)) for i in range(8)]

        d_cond = sem("d_cond")
        d_x = [sem(f"d_x{t}") for t in range(NB * TT)]
        d_ln1 = [sem(f"d_ln1_{k}") for k in range(KT)]
        d_att = [sem(f"d_att{k}") for k in range(KT)]
        d_ln2 = [sem(f"d_ln2_{k}") for k in range(2)]
        d_gate = [sem(f"d_gate{k}") for k in range(2)]
        d_ffn = [sem(f"d_ffn{c}") for c in range(C)]
        d_small = sem("d_small")
        d_out = sem("d_out")
        zeroed = sem("zeroed")
        tail_zero = sem("tail_zero")
        ident_z = sem("ident_z")
        ident_ok = sem("ident_ok")
        consts_ok = sem("consts_ok")
        sel_ok = sem("sel_ok")
        selb_ok = sem("selb_ok")
        silu_c = sem("silu_c")
        rows_done = sem("rows_done")
        rows_copied = sem("rows_copied")
        cols_done = sem("cols_done")
        modc_ok = sem("modc_ok")
        gate_done = sem("gate_done")
        gate_a = sem("gate_a")
        gate_s = sem("gate_s")
        gate_m = sem("gate_m")
        gate_ok = sem("gate_ok")
        msum_ok = sem("msum_ok")
        blk_done = sem("blk_done")
        keep_ok = sem("keep_ok")
        masked = sem("masked")
        w_hi = sem("w_hi")
        w_lo = sem("w_lo")
        bn_done = sem("bn_done")
        stats_ok = sem("stats_ok")
        veps_ok = sem("veps_ok")
        rstd_ok = sem("rstd_ok")
        xn_ok = sem("xn_ok")
        xt_done = sem("xt_done")
        h_ok = sem("h_ok")
        h_hi = sem("h_hi")
        h_lo = sem("h_lo")
        att_done = sem("att_done")
        att_read = sem("att_read")
        x1_ok = sem("x1_ok")
        checked = sem("checked")
        flagv_ok = sem("flagv_ok")
        flag_done = sem("flag_done")
        flag_ok = sem("flag_ok")
        wgu_hi = sem("wgu_hi")
        wd_hi = sem("wd_hi")
        gate_mm = sem("gate_mm")
        up_mm = sem("up_mm")
        silu_ok = sem("silu_ok")
        inner_ok = sem("inner_ok")
        in_hi = sem("in_hi")
        in_lo = sem("in_lo")
        down_mm = sem("down_mm")
        acc_mm = sem("acc_mm")
        acc_read = sem("acc_read")
        out_ok = sem("out_ok")

        def wait_down(eng, s):
            if s % C == C - 1:
                eng.wait_ge(acc_mm, TT * (s // C + 1))
            else:
                eng.wait_ge(down_mm, s - s // C + 1)

        block = ctx.enter_context(nc.Block())

        @block.sync
        def _(sp):
            sp.dma_start(condt[:, :, :], cond).then_inc(d_cond, 16)
            for t in range(TT):
                sp.dma_start(xt[:, t, :], x[t * P:(t + 1) * P, :]).then_inc(d_x[t], 16)

            def load_ln1(k):
                sp.dma_start(modw[:, k // 2, 2 * (k % 2):2 * (k % 2) + 2, :], mod_ln1[k])\
                  .then_inc(d_ln1[k], 16)
                sp.dma_start(awork[:, k, :], att_w[k * P:(k + 1) * P, :]).then_inc(d_att[k], 16)
                sp.dma_start(maskt[:, k, :], att_mask[k * P:(k + 1) * P, :]).then_inc(d_att[k], 16)

            for k in range(KT - 1):
                load_ln1(k)
            for t in range(TT, 2 * TT):
                sp.dma_start(xt[:, t, :], x[t * P:(t + 1) * P, :]).then_inc(d_x[t], 16)
            load_ln1(KT - 1)
            sp.dma_start(modw[:, 2, :, :], mod_gate[0]).then_inc(d_gate[0], 16)
            for h in range(2):
                sp.wait_ge(rows_done, 2 * h + 2)
                sp.dma_start(modw[:, h, :, :], mod_ln2[h]).then_inc(d_ln2[h], 16)
            for c in range(C):
                if c < C - 1:
                    sp.dma_start(wffn[:, c, 0:2 * D], w_gu[c]).then_inc(d_ffn[c], 16)
                    sp.dma_start(raw_d(c), w_down[c * P:(c + 1) * P, :]).then_inc(d_ffn[c], 16)
                else:
                    sp.wait_ge(tail_zero, 1)
                    sp.dma_start(wffn[:, c, 0:2 * D].rearrange("p (n i) -> p n i", i=P)[:, :, 0:FT],
                                 w_gu_tail).then_inc(d_ffn[c], 16)
                    sp.dma_start(wffn[0:FT, c, 2 * D:3 * D], w_down[c * P:F, :])\
                      .then_inc(d_ffn[c], 16)
                if c == 4:
                    sp.wait_ge(rows_done, KT + 1)
                    sp.dma_start(modw[:, 2, :, :], mod_gate[1]).then_inc(d_gate[1], 16)
            for n in range(NB * TT):
                sp.wait_ge(out_ok, n + 1)
                sp.dma_start(out[n * P:(n + 1) * P, :], xt[:, n, :]).then_inc(d_out, 16)
            sp.wait_ge(d_out, 16 * NB * TT)

        @block.gpsimd
        def _(pool):
            pool.memset(ident[:, :], 0.0).then_inc(ident_z, 1)
            pool.memset(mhalf[:, :], -0.5).then_inc(ident_z, 1)
            pool.wait_ge(ident_z, 2)
            pool.affine_select(out=ident[:, :], in_=ident[:, :], compare_op=ALU.not_equal, fill=1.0,
                               base=0, pattern=[[-1, P]], channel_multiplier=1).then_inc(ident_ok, 1)

            def inverse_deviation(q):
                pool.wait_ge(stats_ok, TT * (q + 1))
                pool.tensor_scalar(veps[:, q, :], mv[:, q, :, 1], EPS, None, ALU.add)\
                    .then_inc(veps_ok, 1)
                pool.wait_ge(veps_ok, q + 1)
                pool.tensor_tensor(rstd[:, q, :], veps[:, q, :], mhalf[:, :], ALU.pow)\
                    .then_inc(rstd_ok, 1)

            def mask_weights(k):
                pool.wait_ge(d_att[k], 32)
                pool.wait_ge(keep_ok, k + 1)
                w = awork[:, k, :].rearrange("p (b i) -> p b i", i=BLK)
                pool.tensor_tensor(w, w, keep[:, k, :].unsqueeze(2).to_broadcast([P, NBLK, BLK]),
                                   ALU.mult).then_inc(masked, 1)
                pool.wait_ge(masked, k + 1)
                pool.wait_ge(w_hi, k + 1)
                pool.tensor_tensor(wsplit[:, 2 * k + 1, :], awork[:, k, :],
                                   wsplit[:, 2 * k, :].bitcast(F32), ALU.subtract).then_inc(w_lo, 1)

            def add_to_x(b, t):
                n = b * TT + t
                pool.wait_ge(att_read, n + 1)
                pool.tensor_tensor(xt[:, n, :], xt[:, n, :], xn[:, t, :], ALU.add).then_inc(x1_ok, 1)

            inverse_deviation(0)
            for k in range(KT):
                mask_weights(k)
                if k == KT - 2:
                    inverse_deviation(1)
            for b in range(NB):
                for t in range(TT):
                    add_to_x(b, t)
                inverse_deviation(2 + b)
            for t in range(TT):
                pool.wait_ge(acc_read, t + 1)
                pool.tensor_tensor(xt[:, t, :], xt[:, t, :], xn[:, t, :], ALU.add)\
                    .then_inc(out_ok, 1)

        @block.scalar
        def _(act):
            act.dma_start(scal[:, 0:C - 1, :], scales).then_inc(d_small, 16)
            act.wait_ge(zeroed, 2)
            act.dma_start(scal[0:FT, C - 1, :], scales_tail).then_inc(d_small, 16)
            act.dma_start(adb[:, :], down_scale.to_broadcast([P, D])).then_inc(d_small, 16)

            act.wait_ge(d_cond, 16)
            act.wait_ge(zeroed, 3)
            act.activation(sc[:, :, 0:NB], condt[:, :, :], ACT.Silu).then_inc(silu_c, 1)

            ROWS_BANK = [6, 6, 6, 6, 6, 2, 2, 3]
            ROWS_SLOT = [0, 1, 0, 1, 2, 0, 1, 2]

            def copy_rows(n):
                w = D // 2 if n < KT else D
                act.wait_ge(rows_done, n + 1)
                if n in (2, 3):
                    act.wait_ge(cols_done, n - 1)
                elif n in (5, 6):
                    act.wait_ge(cols_done, KT)
                elif n == 7:
                    act.wait_ge(gate_done, 2)
                act.activation(rows[:, ROWS_SLOT[n], 0:w], bank[ROWS_BANK[n]][:, 0:w], ACT.Copy)\
                   .then_inc(rows_copied, 1)

            def modulate(n):
                q, k = divmod(n, KT)
                layer, b = divmod(q, NB)
                act.wait_ge(xt_done, n + 1)
                act.wait_ge(modc_ok, k + 1 if layer == 0 else KT + 1 + k // 2)
                if n >= 2:
                    act.wait_ge(h_lo, n - 1)
                src = bank[4 + n % 2] if q < 2 else bank[n % 2] if q == 2 else bank[3]
                act.activation(hbuf[:, n % 2, :], src[:, :], ACT.Identity,
                               bias=modc[:, layer, k, 2 + b:3 + b],
                               scale=modc[:, layer, k, b:b + 1]).then_inc(h_ok, 1)

            def round_att(k):
                act.wait_ge(masked, k + 1)
                act.activation(wsplit[:, 2 * k, :], awork[:, k, :], ACT.Copy).then_inc(w_hi, 1)

            def check_chunk(c):
                act.wait_ge(d_ffn[c], 32)
                if c == C - 1:
                    act.wait_ge(tail_zero, 1)
                if c:
                    act.wait_ge(checked, c)
                low = wffn[:, c, :].bitcast(U16).rearrange("p (n h) -> p n h", h=2)[:, :, 0]
                act.activation(junk[:, :], low, ACT.Copy, accum_out=chk[:, c:c + 1])\
                   .then_inc(checked, 1)

            def round_gu(s):
                act.wait_ge(d_ffn[s % C], 32)
                if s >= 2:
                    act.wait_ge(up_mm, s - 1)
                act.activation(whi_gu[:, s % 2, :], wffn[:, s % C, 0:2 * D], ACT.Copy)\
                   .then_inc(wgu_hi, 1)

            def round_d(s):
                if s >= 3:
                    wait_down(act, s - 3)
                act.activation(whi_d(s), raw_d(s % C), ACT.Copy).then_inc(wd_hi, 1)

            for k in range(KT):
                copy_rows(k)
                modulate(k)
                round_att(k)
            for n in range(4, 8):
                modulate(n)
                if n == 5:
                    copy_rows(4)
            check_at = iter(range(C))
            copy_rows(5)
            copy_rows(6)
            for _ in range(GROUPS[0][1]):
                check_chunk(next(check_at))
            round_gu(0)
            for n in range(8, 12):
                modulate(n)
            for s in range(STEPS):
                if s + 1 < STEPS:
                    round_gu(s + 1)
                act.wait_ge(gate_mm, s + 1)
                if s == 0:
                    act.wait_ge(d_small, 48)
                if s >= 2:
                    act.wait_ge(inner_ok, s - 1)
                act.activation(silu_g[:, s % 2, :], bank[gu_bank(s, 0)][:, :], ACT.Silu,
                               scale=scal[:, s % C, 0:1]).then_inc(silu_ok, 1)
                round_d(s)
                for _ in range(CHECKS_AT.get(s, 0)):
                    c = next(check_at, None)
                    if c is not None:
                        check_chunk(c)
                if s == 3:
                    copy_rows(7)
                if 6 <= s < 10:
                    modulate(6 + s)

        @block.vector
        def _(dve):
            dve.memset(blkones[:, :], 0.0).then_inc(zeroed, 1)
            dve.memset(scal[:, C - 1, :], 0.0).then_inc(zeroed, 1)
            dve.memset(sc[:, :, :], 0.0).then_inc(zeroed, 1)
            dve.memset(oneplus[:, :], 0.0).then_inc(zeroed, 1)
            dve.wait_ge(zeroed, 4)
            for g in range(P // BLK):
                s = slice(g * BLK, (g + 1) * BLK)
                dve.memset(blkones[s, s], 1.0).then_inc(consts_ok, 1)
            dve.memset(onecol[:, :], 1.0).then_inc(consts_ok, 1)
            ones = oneplus[:, :].rearrange("p (g v b) -> p g v b", g=2, v=2)[:, :, 0, :]
            dve.memset(ones, 1.0).then_inc(consts_ok, 1)
            dve.memset(wffn[:, C - 1, :], 0.0).then_inc(tail_zero, 1)
            dve.wait_ge(ident_ok, 1)
            dve.tensor_reduce(sel[:, :], ident[:, :].rearrange("p (j r) -> p r j", r=BLK)[:, 0:NB, :],
                              AX_X, ALU.add).then_inc(sel_ok, 1)
            dve.wait_ge(sel_ok, 1)
            for b in range(NB):
                dve.tensor_copy(selb[:, b, :], sel[:, b:b + 1].to_broadcast([P, P]))\
                   .then_inc(selb_ok, 1)

            def stats(q, t):
                n = q * TT + t
                if q < 2:
                    dve.wait_ge(d_x[n], 16)
                else:
                    dve.wait_ge(x1_ok, n - NB * TT + 1)
                dve.bn_stats(bns[:, q, t, :], xt[:, n % (NB * TT), :]).then_inc(bn_done, 1)
                dve.wait_ge(bn_done, n + 1)
                dve.bn_aggr(mv[:, q, t, :], bns[:, q, t, :]).then_inc(stats_ok, 1)

            def normalise(q):
                dve.wait_ge(rstd_ok, q + 1)
                dve.wait_ge(stats_ok, TT * (q + 1))
                if q:
                    dve.wait_ge(xt_done, TT * q)
                if q >= 2:
                    dve.wait_ge(x1_ok, TT * (q - 1))
                for t in range(TT):
                    dve.tensor_scalar(xn[:, t, :], xt[:, q % NB * TT + t, :], mv[:, q, t, 0:1],
                                      rstd[:, q, t:t + 1], ALU.subtract, ALU.mult).then_inc(xn_ok, 1)

            def sum_mask(k):
                dve.wait_ge(d_att[k], 32)
                dve.tensor_reduce(msum[:, k, :], maskt[:, k, :].rearrange("p (b i) -> p b i", i=BLK),
                                  AX_X, ALU.add).then_inc(msum_ok, 1)

            def keep_blocks(k):
                dve.wait_ge(blk_done, k + 1)
                dve.tensor_scalar(keep[:, k, :], bank[7][:, 0:NBLK], 0.0, None, ALU.is_gt)\
                   .then_inc(keep_ok, 1)

            def mod_columns(n):
                dve.wait_ge(cols_done, n + 1)
                dve.wait_ge(consts_ok, 6)
                if n < KT:
                    dve.tensor_tensor(modc[:, 0, n, :], bank[7][:, 0:4], oneplus[:, 0:4], ALU.add)\
                       .then_inc(modc_ok, 1)
                else:
                    k = 2 * (n - KT)
                    dve.tensor_tensor(modc[:, 1, k:k + 2, :],
                                      bank[3][:, 0:8].rearrange("p (k v) -> p k v", v=4),
                                      oneplus[:, :].rearrange("p (k v) -> p k v", v=4), ALU.add)\
                       .then_inc(modc_ok, 1)

            def split(n):
                q, k = divmod(n, KT)
                b = q % NB
                dve.wait_ge(h_ok, n + 1)
                if q >= 2:
                    dve.wait_ge(att_done, TT * (b + 1))
                dve.tensor_copy(ht[:, b, k, 0, :], hbuf[:, n % 2, :]).then_inc(h_hi, 1)
                dve.wait_ge(h_hi, n + 1)
                dve.tensor_tensor(ht[:, b, k, 1, :], hbuf[:, n % 2, :],
                                  ht[:, b, k, 0, :].bitcast(F32), ALU.subtract).then_inc(h_lo, 1)

            def guard_gate(n, src):
                dve.wait_ge(gate_done, n + 1)
                dve.wait_ge(msum_ok, KT)
                half_sign, gate = gscr[:, :], gates[:, n, :]
                if n:
                    dve.wait_ge(gate_m, n)
                dve.tensor_scalar(half_sign, src[:, :], 0.0, 0.5, ALU.is_ge, ALU.subtract)\
                   .then_inc(gate_s, 1)
                dve.wait_ge(gate_s, n + 1)
                dve.scalar_tensor_tensor(gate, half_sign, 2.0, src[:, :], ALU.mult, ALU.mult)\
                   .then_inc(gate_a, 1)
                dve.wait_ge(gate_a, n + 1)
                dve.scalar_tensor_tensor(gate, gate, GATE_MIN, half_sign, ALU.max, ALU.mult)\
                   .then_inc(gate_m, 1)
                dve.wait_ge(gate_m, n + 1)
                if n >= 2:
                    dve.wait_ge(d_small, 48)
                    dve.tensor_tensor(gates[:, n, :], gates[:, n, :], adb[:, :], ALU.mult)\
                       .then_inc(gate_ok, 1)

            def gate_linear(b, t):
                n = b * TT + t
                dve.wait_ge(att_done, n + 1)
                dve.wait_ge(gate_m, b + 1)
                dve.wait_ge(xt_done, TT * NB + TT * b)
                if b:
                    dve.wait_ge(x1_ok, TT)
                dve.scalar_tensor_tensor(xn[:, t, :], bank[4 * b + t][:, :], 2.0, gates[:, b, :],
                                         ALU.mult, ALU.mult).then_inc(att_read, 1)

            def flag_vector(g):
                a, z = GROUPS[g]
                dve.wait_ge(checked, z)
                dve.tensor_reduce(flagv[:, g:g + 1], chk[:, a:z], AX_X, ALU.max)\
                   .then_inc(flagv_ok, 1)

            def read_flag(g):
                dve.wait_ge(flag_done, g + 1)
                dve.tensor_scalar(flags[0:1, g:g + 1], bank[3][0:1, 0:1], 0.0, None, ALU.is_gt)\
                   .then_inc(flag_ok, 1)

            def ffn_inner(s):
                c = s % C
                if s == 0:
                    dve.wait_ge(d_small, 48)
                dve.wait_ge(up_mm, s + 1)
                dve.wait_ge(silu_ok, s + 1)
                if s >= 2:
                    dve.wait_ge(in_lo, s - 1)
                dve.scalar_tensor_tensor(inner[:, s % 2, :], bank[gu_bank(s, 1)][:, :],
                                         scal[:, c, 1:2], silu_g[:, s % 2, :],
                                         ALU.mult, ALU.mult).then_inc(inner_ok, 1)
                dve.wait_ge(inner_ok, s + 1)
                if s >= 3:
                    wait_down(dve, s - 3)
                hi, lo = wsplit[:, 2 * (s % 3), :], wsplit[:, 2 * (s % 3) + 1, :]
                dve.tensor_copy(hi, inner[:, s % 2, :]).then_inc(in_hi, 1)
                dve.wait_ge(in_hi, s + 1)
                dve.tensor_tensor(lo, inner[:, s % 2, :], hi.bitcast(F32), ALU.subtract)\
                   .then_inc(in_lo, 1)

            def gate_ffn(b, t):
                n = b * TT + t
                dve.wait_ge(acc_mm, n + 1)
                dve.wait_ge(gate_ok, b + 1)
                dve.wait_ge(xt_done, 4 * TT)
                if b:
                    dve.wait_ge(out_ok, TT)
                dve.scalar_tensor_tensor(xn[:, t, :], bank[4 + t][:, :], 2.0, gates[:, 2 + b, :],
                                         ALU.mult, ALU.mult).then_inc(acc_read, 1)

            for t in range(TT):
                stats(0, t)
            normalise(0)
            mod_columns(0)
            sum_mask(0)
            keep_blocks(0)
            for k in range(KT):
                split(k)
                if k + 1 < KT:
                    mod_columns(k + 1)
                    sum_mask(k + 1)
                    keep_blocks(k + 1)
                if k == 1:
                    for t in range(TT):
                        stats(1, t)
                if k == 2:
                    normalise(1)
            split(4)
            split(5)
            guard_gate(0, bank[6])
            gate_linear(0, 0)
            gate_linear(0, 1)
            gate_linear(0, 2)
            gate_linear(0, 3)
            split(6)
            stats(2, 0)
            stats(2, 1)
            split(7)
            stats(2, 2)
            stats(2, 3)
            mod_columns(4)
            mod_columns(5)
            normalise(2)
            guard_gate(1, bank[2])
            flag_vector(0)
            read_flag(0)
            for n in range(8, 12):
                split(n)
            for s in range(STEPS):
                if s == 0:
                    for t in range(TT):
                        gate_linear(1, t)
                if s == 2:
                    read_flag(1)
                if s == 5:
                    guard_gate(3, bank[3])
                    read_flag(2)
                ffn_inner(s)
                if s == 0:
                    stats(3, 0)
                    stats(3, 1)
                if s == 1:
                    stats(3, 2)
                    stats(3, 3)
                    flag_vector(1)
                if s == 2:
                    normalise(3)
                if s == 4:
                    guard_gate(2, bank[3])
                    flag_vector(2)
                if 6 <= s < 10:
                    split(6 + s)
                if s == C + LAG - 1:
                    for t in range(TT):
                        gate_ffn(0, t)
            for t in range(TT):
                n = TT + t
                gate_ffn(1, t)
                dve.wait_ge(acc_read, n + 1)
                dve.tensor_tensor(xt[:, n, :], xt[:, n, :], xn[:, t, :], ALU.add).then_inc(out_ok, 1)

        @block.tensor
        def _(pe):
            def mod_rows(n, w, src, dst):
                if n == 0:
                    pe.wait_ge(silu_c, 1)
                for j in range(KT):
                    last = pe.matmul(dst[32 * j:32 * (j + 1), 0:w], sc[:, j, :], src(j), start=True, stop=True)
                last.then_inc(rows_done, 1)

            def rows_ln1(k):
                pe.wait_ge(d_ln1[k], 16)
                if k:
                    pe.wait_ge(rows_copied, k)
                m = modw[:, k // 2, 2 * (k % 2):2 * (k % 2) + 2, :].rearrange("p a n -> p (a n)")
                mod_rows(k, D // 2, lambda j: m[:, j * (D // 2):(j + 1) * (D // 2)], bank[6])

            def columns(n, slot, ntile, dst):
                pe.wait_ge(sel_ok, 1)
                for i in range(ntile * 2):
                    last = pe.matmul(dst[:, NB * i:NB * (i + 1)], rows[:, slot, i * P:(i + 1) * P],
                                     sel[:, :], start=True, stop=True)
                last.then_inc(cols_done, 1)

            def columns_ln1(k):
                pe.wait_ge(rows_copied, k + 1)
                if k:
                    pe.wait_ge(keep_ok, k)
                columns(k, k % 2, 1, bank[7])

            def mask_blocks(k):
                pe.wait_ge(msum_ok, k + 1)
                pe.wait_ge(consts_ok, 6)
                pe.wait_ge(modc_ok, k + 1)
                pe.matmul(bank[7][:, 0:NBLK], blkones[:, :], msum[:, k, :], start=True, stop=True)\
                  .then_inc(blk_done, 1)

            def transposes(n):
                q, k = divmod(n, KT)
                dst = bank[4 + n % 2] if q < 2 else bank[n % 2] if q == 2 else bank[3]
                if k == 0:
                    pe.wait_ge(xn_ok, TT * (q + 1))
                if q == 2 and k < 2:
                    pe.wait_ge(att_read, k + 1)
                elif q == 3:
                    pe.wait_ge(h_ok, n)
                elif n >= 2:
                    pe.wait_ge(h_ok, n - 1)
                for t in range(TT):
                    last = pe.transpose(dst[:, t * P:(t + 1) * P], xn[:, t, k * P:(k + 1) * P],
                                        ident[:, :])
                last.then_inc(xt_done, 1)

            def linear(b, k, t):
                if t == 0:
                    pe.wait_ge(h_lo, TT * b + k + 1)
                    if b == 0:
                        pe.wait_ge(w_lo, k + 1)
                if b == 1 and k == 0:
                    if t < 2:
                        pe.wait_ge(h_ok, 7 + t)
                    elif t == 2:
                        pe.wait_ge(gate_a, 1)
                    else:
                        pe.wait_ge(keep_ok, KT)
                for part in range(2):
                    for wpart in range(2):
                        last = pe.matmul(bank[4 * b + t][:, :],
                                         ht[:, b, k, part, t * P:(t + 1) * P],
                                         wsplit[:, 2 * k + wpart, :],
                                         start=(k == 0 and part == 0 and wpart == 0),
                                         stop=(k == KT - 1 and part == 1 and wpart == 1))
                if k == KT - 1:
                    last.then_inc(att_done, 1)

            def gate_all(b, slot, dst):
                pe.wait_ge(selb_ok, NB)
                pe.matmul(dst[:, :], selb[:, b, :], rows[:, slot, :], start=True, stop=True)\
                  .then_inc(gate_done, 1)

            def flag_sum(g):
                pe.wait_ge(flagv_ok, g + 1)
                pe.matmul(bank[3][0:1, 0:1], flagv[:, g:g + 1], onecol[:, :], start=True, stop=True)\
                  .then_inc(flag_done, 1)

            general = []

            def load_flag(g):
                pe.wait_ge(flag_ok, g + 1)
                general.append(pe.value_load(flags[0:1, g:g + 1], min_val=0, max_val=1))

            def gate_up(s):
                b, c = divmod(s, C)
                pe.wait_ge(wgu_hi, s + 1)

                def products(u, k, native):
                    dst = bank[gu_bank(s, u)]
                    if c == 0 and u == 0:
                        pe.wait_ge(h_lo, TT * (2 + b) + k + 1)
                    w = whi_gu[:, s % 2, (u * KT + k) * P:(u * KT + k + 1) * P]
                    for part in range(2):
                        h = ht[:, b, k, part, :]
                        if native:
                            w, h = raw_gu(c, u, k), h.bitcast(F32)
                        last = pe.matmul(dst[:, :], w, h, start=(k == 0 and part == 0),
                                         stop=(k == KT - 1 and part == 1))
                    return last

                if s == 0:
                    pe.wait_ge(gate_a, 2)
                elif s == 1:
                    pe.wait_ge(h_ok, 12)
                else:
                    pe.wait_ge(inner_ok, s - 1)
                yes = general[GROUP_OF[c]]
                with pe.If(yes):
                    for k in range(KT):
                        last = products(0, k, True)
                    last.then_inc(gate_mm, 1)
                with pe.Else():
                    for k in range(KT):
                        last = products(0, k, False)
                    last.then_inc(gate_mm, 1)
                if s == 0:
                    pe.wait_ge(h_ok, 11)
                else:
                    pe.wait_ge(silu_ok, s)
                with pe.If(yes):
                    for k in range(KT):
                        last = products(1, k, True)
                    last.then_inc(up_mm, 1)
                with pe.Else():
                    for k in range(KT):
                        last = products(1, k, False)
                    last.then_inc(up_mm, 1)

            def down(s):
                b, c = divmod(s, C)
                pe.wait_ge(in_lo, s + 1)
                pe.wait_ge(wd_hi, s + 1)

                def products(t, native):
                    for part in range(2):
                        h = wsplit[:, 2 * (s % 3) + part, t * P:(t + 1) * P]
                        w = whi_d(s)
                        if native:
                            h, w = h.bitcast(F32), raw_d(c)
                        last = pe.matmul(bank[4 + t][:, :], h, w, start=(c == 0 and part == 0),
                                         stop=(c == C - 1 and part == 1))
                    if c == C - 1:
                        last.then_inc(acc_mm, 1)
                    elif t == TT - 1:
                        last.then_inc(down_mm, 1)

                if c == 0:
                    if b == 0:
                        pe.wait_ge(att_read, 2 * TT)
                    else:
                        pe.wait_ge(acc_read, TT)
                with pe.If(general[GROUP_OF[c]]):
                    for t in range(TT):
                        products(t, True)
                with pe.Else():
                    for t in range(TT):
                        products(t, False)

            rows_ln1(0)
            columns_ln1(0)
            mask_blocks(0)
            pe.wait_ge(ident_ok, 1)
            for n in range(3):
                transposes(n)
            for k in range(KT):
                linear(0, k, 0)
                if k == KT - 1:
                    transposes(4)
                    transposes(5)
                    pe.wait_ge(d_gate[0], 16)
                    pe.wait_ge(rows_copied, 4)
                    mod_rows(4, D, lambda j: modw[:, 2, j, :], bank[6])
                else:
                    rows_ln1(k + 1)
                linear(0, k, 1)
                if k == KT - 1:
                    transposes(6)
                else:
                    columns_ln1(k + 1)
                linear(0, k, 2)
                if k == KT - 1:
                    transposes(7)
                    pe.wait_ge(rows_copied, 5)
                    gate_all(0, 2, bank[6])
                else:
                    mask_blocks(k + 1)
                linear(0, k, 3)
                if k == 0:
                    transposes(3)
            for k in range(KT):
                for t in range(TT):
                    linear(1, k, t)
                    if (k, t) == (0, 3):
                        pe.wait_ge(d_ln2[0], 16)
                        pe.wait_ge(att_read, 3)
                        mod_rows(5, D, lambda j: modw[:, 0, j, :], bank[2])
                    if (k, t) == (1, 1):
                        pe.wait_ge(rows_copied, 6)
                        pe.wait_ge(att_read, 4)
                        columns(4, 0, 2, bank[3])
                        pe.wait_ge(d_ln2[1], 16)
                        mod_rows(6, D, lambda j: modw[:, 1, j, :], bank[2])
                    if (k, t) == (2, 0):
                        pe.wait_ge(rows_copied, 7)
                        pe.wait_ge(modc_ok, KT + 1)
                        columns(5, 1, 2, bank[3])
                        gate_all(1, 2, bank[2])
                    if (k, t) == (3, 0):
                        transposes(8)
                        transposes(9)
                    if (k, t) == (3, 2):
                        transposes(10)
            transposes(11)
            pe.wait_ge(modc_ok, KT + 2)
            flag_sum(0)
            load_flag(0)
            for s in range(STEPS + LAG):
                if s == GROUPS[1][0]:
                    load_flag(1)
                if s == GROUPS[2][0]:
                    load_flag(2)
                if s == 5:
                    pe.wait_ge(gate_a, 3)
                    gate_all(1, 2, bank[3])
                if s < STEPS:
                    gate_up(s)
                if s == 2:
                    flag_sum(1)
                if s == 5:
                    pe.wait_ge(gate_a, 4)
                    flag_sum(2)
                if s >= LAG:
                    down(s - LAG)
                if s == 3:
                    pe.wait_ge(d_gate[1], 16)
                    mod_rows(7, D, lambda j: modw[:, 2, j, :], bank[3])
                if s == 4:
                    pe.wait_ge(rows_copied, 8)
                    gate_all(0, 2, bank[3])
                if 6 <= s < 10:
                    transposes(6 + s)


def kernel(L0_attn_data, L0_attn_weight, L0_attn_mask, L0_ffn_Wg, L0_ffn_Wu, L0_ffn_Wd, L0_ffn_ag,
           L0_ffn_au, L0_ffn_ad, L0_c, L0_wmod):
    import numpy as np
    from concourse import bacc
    from concourse.bass_utils import run_bass_kernel_spmd

    def c_(a):
        return np.ascontiguousarray(a)

    x = np.asarray(L0_attn_data)
    shape = x.shape
    nf = C - 1
    wmod = np.asarray(L0_wmod).reshape(KT, P, 6, D)

    def ln_weights(scale, shift):
        w = wmod[:, :, [scale, shift], :].reshape(KT, P, 2, KT, P)
        return w.transpose(3, 1, 0, 2, 4)

    gu = np.stack([np.asarray(L0_ffn_Wg), np.asarray(L0_ffn_Wu)])
    gu_full = gu[:, :nf * P].reshape(2, nf, P, KT, P).transpose(1, 4, 0, 3, 2)
    gu_tail = gu[:, nf * P:].reshape(2, FT, KT, P).transpose(3, 0, 2, 1)
    sc = np.stack([np.asarray(L0_ffn_ag), np.asarray(L0_ffn_au)])
    ln2 = ln_weights(4, 3).reshape(2, 2, P, KT, 2 * P).transpose(0, 2, 3, 1, 4)
    arrays = {
        "x": c_(x.reshape(NB * SEQ, D)),
        "att_w": c_(np.asarray(L0_attn_weight).T),
        "att_mask": c_(np.asarray(L0_attn_mask).T),
        "cond": c_(np.asarray(L0_c).T.reshape(KT, P, NB).transpose(1, 0, 2)),
        "mod_ln1": c_(ln_weights(1, 0).reshape(KT, P, 2, D)),
        "mod_ln2": c_(ln2.reshape(2, P, KT, D)),
        "mod_gate": c_(wmod[:, :, [2, 5], :].transpose(2, 1, 0, 3)),
        "w_gu": c_(gu_full.reshape(nf, P, 2 * D)),
        "w_gu_tail": c_(gu_tail.reshape(P, 2 * KT, FT)),
        "w_down": c_(np.asarray(L0_ffn_Wd).T),
        "scales": c_(sc[:, :nf * P].reshape(2, nf, P).transpose(2, 1, 0)),
        "scales_tail": c_(sc[:, nf * P:].T),
        "down_scale": c_(np.asarray(L0_ffn_ad).reshape(1, D)),
    }
    nc = bacc.Bacc("TRN2", target_bir_lowering=False, num_devices=1)
    args = [nc.dram_tensor(f"in_{name}", a.shape, mybir.dt.from_np(a.dtype), kind="ExternalInput").ap()
            for name, a in arrays.items()]
    args.append(nc.dram_tensor("out_0", (NB * SEQ, D), F32, kind="ExternalOutput").ap())
    adaln_block(nc, *args)
    r = run_bass_kernel_spmd(nc, [{f"in_{name}": a for name, a in arrays.items()}], core_ids=[0])
    return r.results[0]["out_0"].reshape(shape)
```

```python
from contextlib import ExitStack

import concourse.bass as bass
from concourse import mybir

F32 = mybir.dt.float32
F32R = mybir.dt.float32r
I32 = mybir.dt.int32
U16 = mybir.dt.uint16
U8 = mybir.dt.uint8
ALU = mybir.AluOpType
ACT = mybir.ActivationFunctionType
AX_X = mybir.AxisListType.X

P = 128
D = 512
KT = D // P
NB = 2
TT = 4
SEQ = TT * P
F = 1376
C = -(-F // P)
FT = F - (C - 1) * P
BLK = 32
NBLK = D // BLK
EPS = 1e-5
GATE_MIN = 0.25
STEPS = NB * C
WARM_UP = 22
LAG = 2
CHECKS_AT = {0: 1, 1: 1, 2: 2, 3: 2, 4: 1}
GROUPS = [(0, 3), (3, 6), (6, C)]
GROUP_OF = [g for g, (a, b) in enumerate(GROUPS) for _ in range(a, b)]


def gu_bank(s, u):
    return (2 * s + u + 2) % 3


def adaln_block(nc, x, att_w, att_mask, cond, mod_ln1, mod_ln2, mod_gate, w_gu, w_gu_tail, w_down,
                scales, scales_tail, down_scale, out):
    with ExitStack() as ctx:
        def sb(name, shape, dt=F32):
            return ctx.enter_context(nc.sbuf_tensor(name, shape, dt))

        def sem(name):
            return ctx.enter_context(nc.semaphore(name))

        xt = sb("xt", [P, NB * TT, D])
        xn = sb("xn", [P, TT, D])
        ht = sb("ht", [P, NB, KT, 2, SEQ], F32R)
        hbuf = sb("hbuf", [P, 2, SEQ])
        awork = sb("awork", [P, KT, D])
        maskt = sb("maskt", [P, KT, D], I32)
        wsplit = sb("wsplit", [P, KT * 2, D], F32R)
        modw = sb("modw", [P, 3, KT, D])
        rows = sb("rows", [P, 3, D])
        wffn = sb("wffn", [P, C, 3 * D])
        whi_gu = sb("whi_gu", [P, 2, 2 * D], F32R)
        whi_d2 = sb("whi_d2", [P, D], F32R)
        junk = sb("junk", [P, 3 * D], U8)
        scal = sb("scal", [P, C, 2])
        adc = sb("adc", [P, KT])
        gcol = sb("gcol", [P, 2, KT, NB])
        gscr = sb("gscr", [P, 2, KT, NB])
        condt = sb("condt", [P, KT, NB])
        sc = sb("sc", [P, KT, BLK])
        ident = sb("ident", [P, P])
        blkones = sb("blkones", [P, P])
        sel = sb("sel", [P, NB])
        oneplus = sb("oneplus", [P, 8])
        onecol = sb("onecol", [P, 1])
        msum = sb("msum", [P, KT, NBLK])
        keep = sb("keep", [P, KT, NBLK])
        modc = sb("modc", [P, 2, KT, 4])
        bns = sb("bns", [P, 2 * NB, TT, 6])
        mv = sb("mv", [P, 2 * NB, TT, 2])
        veps = sb("veps", [P, 2 * NB, TT])
        rstd = sb("rstd", [P, 2 * NB, TT])
        mhalf = sb("mhalf", [P, TT])
        chk = sb("chk", [P, C])
        flagv = sb("flagv", [P, len(GROUPS)])
        flags = sb("flags", [1, len(GROUPS)], I32)

        gates = maskt[:, :, :].bitcast(F32)
        silu_g = awork[:, 0:2, :]
        inner = awork[:, 2:4, :]

        def raw_gu(c, u, k):
            return wffn[:, c, (u * KT + k) * P:(u * KT + k + 1) * P]

        def raw_d(c):
            return wffn[:, c, 2 * D:3 * D]

        def whi_d(s):
            return wsplit[:, 6 + s % 3, :] if s % 3 < 2 else whi_d2[:, :]

        bank = [ctx.enter_context(nc.psum_tensor(f"bank{i}", [P, D], F32)) for i in range(8)]

        d_cond = sem("d_cond")
        d_x = [sem(f"d_x{t}") for t in range(NB * TT)]
        d_ln1 = [sem(f"d_ln1_{k}") for k in range(KT)]
        d_att = [sem(f"d_att{k}") for k in range(KT)]
        d_mask = [sem(f"d_mask{k}") for k in range(KT)]
        d_ln2 = [sem(f"d_ln2_{k}") for k in range(2)]
        d_gate = [sem(f"d_gate{k}") for k in range(2)]
        d_ffn = [sem(f"d_ffn{c}") for c in range(C)]
        d_small = sem("d_small")
        d_out = sem("d_out")
        zeroed = sem("zeroed")
        tail_zero = sem("tail_zero")
        ident_z = sem("ident_z")
        ident_ok = sem("ident_ok")
        consts_ok = sem("consts_ok")
        sel_ok = sem("sel_ok")
        silu_c = sem("silu_c")
        rows_done = sem("rows_done")
        rows_copied = sem("rows_copied")
        cols_done = sem("cols_done")
        modc_ok = sem("modc_ok")
        gate_s = sem("gate_s")
        gate_a = sem("gate_a")
        gate_m = sem("gate_m")
        gcol_ok = sem("gcol_ok")
        gate_done = sem("gate_done")
        gate_ok = sem("gate_ok")
        msum_ok = sem("msum_ok")
        blk_done = sem("blk_done")
        keep_ok = sem("keep_ok")
        masked = sem("masked")
        w_hi = sem("w_hi")
        w_lo = sem("w_lo")
        bn_done = sem("bn_done")
        stats_ok = sem("stats_ok")
        veps_ok = sem("veps_ok")
        rstd_ok = sem("rstd_ok")
        xn_ok = sem("xn_ok")
        xt_done = sem("xt_done")
        h_ok = sem("h_ok")
        h_hi = [sem(f"h_hi{q}") for q in range(2 * NB)]
        h_lo = [sem(f"h_lo{q}") for q in range(2 * NB)]
        att_done = sem("att_done")
        att_read = sem("att_read")
        x1_ok = sem("x1_ok")
        checked = sem("checked")
        flagv_ok = sem("flagv_ok")
        flag_done = sem("flag_done")
        flag_ok = sem("flag_ok")
        wgu_hi = sem("wgu_hi")
        wd_hi = sem("wd_hi")
        gate_mm = sem("gate_mm")
        up_mm = sem("up_mm")
        silu_ok = sem("silu_ok")
        inner_ok = sem("inner_ok")
        in_hi = sem("in_hi")
        in_lo = sem("in_lo")
        down_mm = sem("down_mm")
        acc_mm = sem("acc_mm")
        acc_read = sem("acc_read")
        out_ok = sem("out_ok")

        def wait_split(eng, n):
            eng.wait_ge(h_lo[n // KT], n % KT + 1)

        def wait_down(eng, s):
            if s % C == C - 1:
                eng.wait_ge(acc_mm, TT * (s // C + 1))
            else:
                eng.wait_ge(down_mm, s - s // C + 1)

        block = ctx.enter_context(nc.Block())

        @block.sync
        def _(sp):
            sp.dma_start(condt[:, :, :], cond).then_inc(d_cond, 16)
            for t in range(TT):
                sp.dma_start(xt[:, t, :], x[t * P:(t + 1) * P, :]).then_inc(d_x[t], 16)

            def load_att(k):
                sp.dma_start(maskt[:, k, :], att_mask[k * P:(k + 1) * P, :]).then_inc(d_mask[k], 16)
                sp.dma_start(modw[:, k // 2, 2 * (k % 2):2 * (k % 2) + 2, :], mod_ln1[k])\
                  .then_inc(d_ln1[k], 16)
                sp.dma_start(awork[:, k, :], att_w[k * P:(k + 1) * P, :]).then_inc(d_att[k], 16)

            def load_x(t):
                sp.dma_start(xt[:, t, :], x[t * P:(t + 1) * P, :]).then_inc(d_x[t], 16)

            for k in range(KT - 1):
                load_att(k)
            load_x(TT)
            load_x(TT + 1)
            load_att(KT - 1)
            load_x(TT + 2)
            load_x(TT + 3)
            sp.dma_start(modw[:, 2, :, :], mod_gate[0]).then_inc(d_gate[0], 16)
            sp.wait_ge(rows_done, 2)
            sp.dma_start(modw[:, 0, :, :], mod_ln2[0]).then_inc(d_ln2[0], 16)
            for c in range(C):
                if c == 1:
                    sp.wait_ge(rows_done, 4)
                    sp.dma_start(modw[:, 1, :, :], mod_ln2[1]).then_inc(d_ln2[1], 16)
                if c < C - 1:
                    sp.dma_start(wffn[:, c, 0:2 * D], w_gu[c]).then_inc(d_ffn[c], 16)
                    sp.dma_start(raw_d(c), w_down[c * P:(c + 1) * P, :]).then_inc(d_ffn[c], 16)
                else:
                    sp.wait_ge(tail_zero, 1)
                    sp.dma_start(wffn[:, c, 0:2 * D].rearrange("p (n i) -> p n i", i=P)[:, :, 0:FT],
                                 w_gu_tail).then_inc(d_ffn[c], 16)
                    sp.dma_start(wffn[0:FT, c, 2 * D:3 * D], w_down[c * P:F, :])\
                      .then_inc(d_ffn[c], 16)
                if c == 4:
                    sp.wait_ge(rows_done, KT + 1)
                    sp.dma_start(modw[:, 2, :, :], mod_gate[1]).then_inc(d_gate[1], 16)
            for n in range(NB * TT):
                sp.wait_ge(out_ok, n + 1)
                sp.dma_start(out[n * P:(n + 1) * P, :], xt[:, n, :]).then_inc(d_out, 16)
            sp.wait_ge(d_out, 16 * NB * TT)

        @block.gpsimd
        def _(pool):
            pool.memset(ident[:, :], 0.0).then_inc(ident_z, 1)
            pool.memset(mhalf[:, :], -0.5).then_inc(ident_z, 1)
            pool.wait_ge(ident_z, 2)
            pool.affine_select(out=ident[:, :], in_=ident[:, :], compare_op=ALU.not_equal, fill=1.0,
                               base=0, pattern=[[-1, P]], channel_multiplier=1).then_inc(ident_ok, 1)

            def inverse_deviation(q):
                pool.wait_ge(stats_ok, TT * (q + 1))
                pool.tensor_scalar(veps[:, q, :], mv[:, q, :, 1], EPS, None, ALU.add)\
                    .then_inc(veps_ok, 1)
                pool.wait_ge(veps_ok, q + 1)
                pool.tensor_tensor(rstd[:, q, :], veps[:, q, :], mhalf[:, :], ALU.pow)\
                    .then_inc(rstd_ok, 1)

            def mask_weights(k):
                pool.wait_ge(d_att[k], 16)
                pool.wait_ge(keep_ok, k + 1)
                w = awork[:, k, :].rearrange("p (b i) -> p b i", i=BLK)
                pool.tensor_tensor(w, w, keep[:, k, :].unsqueeze(2).to_broadcast([P, NBLK, BLK]),
                                   ALU.mult).then_inc(masked, 1)
                pool.wait_ge(masked, k + 1)
                pool.wait_ge(w_hi, k + 1)
                pool.tensor_tensor(wsplit[:, 2 * k + 1, :], awork[:, k, :],
                                   wsplit[:, 2 * k, :].bitcast(F32), ALU.subtract).then_inc(w_lo, 1)

            def add_to_x(b, t):
                n = b * TT + t
                pool.wait_ge(att_read, n + 1)
                pool.tensor_tensor(xt[:, n, :], xt[:, n, :], xn[:, t, :], ALU.add).then_inc(x1_ok, 1)

            def low_part(k):
                pool.wait_ge(h_hi[1], k + 1)
                pool.tensor_tensor(ht[:, 1, k, 1, :], hbuf[:, k % 2, :],
                                   ht[:, 1, k, 0, :].bitcast(F32), ALU.subtract)\
                    .then_inc(h_lo[1], 1)

            inverse_deviation(0)
            for k in range(KT):
                mask_weights(k)
            inverse_deviation(1)
            for k in range(3):
                low_part(k)
            add_to_x(0, 0)
            low_part(3)
            for t in range(1, TT):
                add_to_x(0, t)
            inverse_deviation(2)
            for t in range(TT):
                add_to_x(1, t)
            inverse_deviation(3)
            for t in range(TT):
                pool.wait_ge(acc_read, t + 1)
                pool.tensor_tensor(xt[:, t, :], xt[:, t, :], xn[:, t, :], ALU.add)\
                    .then_inc(out_ok, 1)

        @block.scalar
        def _(act):
            act.dma_start(scal[:, 0:C - 1, :], scales).then_inc(d_small, 16)
            act.dma_start(adc[:, :], down_scale).then_inc(d_small, 16)
            act.wait_ge(zeroed, 2)
            act.dma_start(scal[0:FT, C - 1, :], scales_tail).then_inc(d_small, 16)
            act.wait_ge(d_cond, 16)
            act.wait_ge(zeroed, 3)
            act.activation(sc[:, :, 0:NB], condt[:, :, :], ACT.Silu).then_inc(silu_c, 1)

            ROWS_BANK = [6, 6, 6, 6, 6, 2, 2, 3]
            ROWS_SLOT = [0, 1, 0, 1, 2, 0, 1, 2]
            ROWS_LAST = {2: 0, 3: 1, 5: 2, 6: 3, 7: 4}

            def copy_rows(n):
                w = D // 2 if n < KT else D
                act.wait_ge(rows_done, n + 1)
                if n in ROWS_LAST:
                    act.wait_ge(cols_done, ROWS_LAST[n] + 1)
                act.activation(rows[:, ROWS_SLOT[n], 0:w], bank[ROWS_BANK[n]][:, 0:w], ACT.Copy)\
                   .then_inc(rows_copied, 1)

            def copy_gate(n, src):
                act.wait_ge(gate_done, n + 1)
                act.wait_ge(msum_ok, KT)
                act.activation(gates[:, n, :], src[:, :], ACT.Copy).then_inc(gate_ok, 1)

            def modulate(n):
                q, k = divmod(n, KT)
                layer, b = divmod(q, NB)
                act.wait_ge(xt_done, n + 1)
                act.wait_ge(modc_ok, k + 1 if layer == 0 else KT + 1 + k // 2)
                if n >= 2:
                    wait_split(act, n - 2)
                src = bank[4 + n % 2] if q < 2 else bank[n % 2] if q == 2 else bank[3]
                act.activation(hbuf[:, n % 2, :], src[:, :], ACT.Identity,
                               bias=modc[:, layer, k, 2 + b:3 + b],
                               scale=modc[:, layer, k, b:b + 1]).then_inc(h_ok, 1)

            def round_att(k):
                act.wait_ge(masked, k + 1)
                act.activation(wsplit[:, 2 * k, :], awork[:, k, :], ACT.Copy).then_inc(w_hi, 1)

            def check_chunk(c):
                act.wait_ge(d_ffn[c], 32)
                if c == C - 1:
                    act.wait_ge(tail_zero, 1)
                if c:
                    act.wait_ge(checked, c)
                low = wffn[:, c, :].bitcast(U16).rearrange("p (n h) -> p n h", h=2)[:, :, 0]
                act.activation(junk[:, :], low, ACT.Copy, accum_out=chk[:, c:c + 1])\
                   .then_inc(checked, 1)

            def round_gu(s):
                act.wait_ge(d_ffn[s % C], 32)
                if s >= 2:
                    act.wait_ge(up_mm, s - 1)
                act.activation(whi_gu[:, s % 2, :], wffn[:, s % C, 0:2 * D], ACT.Copy)\
                   .then_inc(wgu_hi, 1)

            def round_d(s):
                if s >= 3:
                    wait_down(act, s - 3)
                act.activation(whi_d(s), raw_d(s % C), ACT.Copy).then_inc(wd_hi, 1)

            for k in range(KT):
                copy_rows(k)
                round_att(k)
                modulate(k)
            check_at = iter(range(C))
            modulate(4)
            copy_rows(4)
            modulate(5)
            copy_gate(0, bank[6])
            modulate(6)
            copy_gate(1, bank[7])
            modulate(7)
            check_chunk(next(check_at))
            copy_rows(5)
            check_chunk(next(check_at))
            copy_rows(6)
            check_chunk(next(check_at))
            check_chunk(next(check_at))
            round_gu(0)
            for n in range(8, 12):
                modulate(n)
            for s in range(STEPS):
                if s + 1 < STEPS:
                    round_gu(s + 1)
                act.wait_ge(gate_mm, s + 1)
                if s == 0:
                    act.wait_ge(d_small, 48)
                if s >= 2:
                    act.wait_ge(inner_ok, s - 1)
                act.activation(silu_g[:, s % 2, :], bank[gu_bank(s, 0)][:, :], ACT.Silu,
                               scale=scal[:, s % C, 0:1]).then_inc(silu_ok, 1)
                round_d(s)
                for _ in range(CHECKS_AT.get(s, 0)):
                    c = next(check_at, None)
                    if c is not None:
                        check_chunk(c)
                if s == 3:
                    copy_rows(7)
                if s == 10:
                    copy_gate(2, bank[3])
                if s == 11:
                    copy_gate(3, bank[3])
                if 6 <= s < 10:
                    modulate(6 + s)

        @block.vector
        def _(dve):
            dve.memset(blkones[:, :], 0.0).then_inc(zeroed, 1)
            dve.memset(scal[:, C - 1, :], 0.0).then_inc(zeroed, 1)
            dve.memset(sc[:, :, :], 0.0).then_inc(zeroed, 1)
            dve.memset(oneplus[:, :], 0.0).then_inc(zeroed, 1)
            dve.wait_ge(zeroed, 4)
            for g in range(P // BLK):
                s = slice(g * BLK, (g + 1) * BLK)
                dve.memset(blkones[s, s], 1.0).then_inc(consts_ok, 1)
            dve.memset(onecol[:, :], 1.0).then_inc(consts_ok, 1)
            ones = oneplus[:, :].rearrange("p (g v b) -> p g v b", g=2, v=2)[:, :, 0, :]
            dve.memset(ones, 1.0).then_inc(consts_ok, 1)
            dve.memset(wffn[:, C - 1, :], 0.0).then_inc(tail_zero, 1)
            dve.wait_ge(ident_ok, 1)
            dve.tensor_reduce(sel[:, :], ident[:, :].rearrange("p (j r) -> p r j", r=BLK)[:, 0:NB, :],
                              AX_X, ALU.add).then_inc(sel_ok, 1)
            def stats(q, t):
                n = q * TT + t
                if q < 2:
                    dve.wait_ge(d_x[n], 16)
                else:
                    dve.wait_ge(x1_ok, n - NB * TT + 1)
                dve.bn_stats(bns[:, q, t, :], xt[:, n % (NB * TT), :]).then_inc(bn_done, 1)
                dve.wait_ge(bn_done, n + 1)
                dve.bn_aggr(mv[:, q, t, :], bns[:, q, t, :]).then_inc(stats_ok, 1)

            def normalise(q):
                dve.wait_ge(rstd_ok, q + 1)
                dve.wait_ge(stats_ok, TT * (q + 1))
                if q:
                    dve.wait_ge(xt_done, TT * q)
                if q >= 2:
                    dve.wait_ge(x1_ok, TT * (q - 1))
                for t in range(TT):
                    dve.tensor_scalar(xn[:, t, :], xt[:, q % NB * TT + t, :], mv[:, q, t, 0:1],
                                      rstd[:, q, t:t + 1], ALU.subtract, ALU.mult).then_inc(xn_ok, 1)

            def sum_mask(k):
                dve.wait_ge(d_mask[k], 16)
                dve.tensor_reduce(msum[:, k, :], maskt[:, k, :].rearrange("p (b i) -> p b i", i=BLK),
                                  AX_X, ALU.add).then_inc(msum_ok, 1)

            def keep_blocks(k):
                dve.wait_ge(blk_done, k + 1)
                dve.tensor_scalar(keep[:, k, :], bank[7][:, 0:NBLK], 0.0, None, ALU.is_gt)\
                   .then_inc(keep_ok, 1)

            def mod_columns(n):
                dve.wait_ge(cols_done, n + 1 if n < KT else n + 2)
                dve.wait_ge(consts_ok, 6)
                if n < KT:
                    dve.tensor_tensor(modc[:, 0, n, :], bank[7][:, 0:4], oneplus[:, 0:4], ALU.add)\
                       .then_inc(modc_ok, 1)
                else:
                    k = 2 * (n - KT)
                    dve.tensor_tensor(modc[:, 1, k:k + 2, :],
                                      bank[7 - n][:, 0:8].rearrange("p (k v) -> p k v", v=4),
                                      oneplus[:, :].rearrange("p (k v) -> p k v", v=4), ALU.add)\
                       .then_inc(modc_ok, 1)

            def split(n):
                q, k = divmod(n, KT)
                b = q % NB
                dve.wait_ge(h_ok, n + 1)
                if q >= 2:
                    dve.wait_ge(att_done, TT * (b + 1))
                dve.tensor_copy(ht[:, b, k, 0, :], hbuf[:, n % 2, :]).then_inc(h_hi[q], 1)
                if q != 1:
                    dve.wait_ge(h_hi[q], k + 1)
                    dve.tensor_tensor(ht[:, b, k, 1, :], hbuf[:, n % 2, :],
                                      ht[:, b, k, 0, :].bitcast(F32), ALU.subtract)\
                       .then_inc(h_lo[q], 1)

            def guard_gate(layer, src):
                dve.wait_ge(cols_done, (KT if layer == 0 else 2 * KT - 1) + 1)
                g = src[:, 0:KT * NB].rearrange("p (k b) -> p k b", b=NB)
                half_sign, gate = gscr[:, layer, :, :], gcol[:, layer, :, :]
                dve.tensor_scalar(half_sign, g, 0.0, 0.5, ALU.is_ge, ALU.subtract)\
                   .then_inc(gate_s, 1)
                dve.wait_ge(gate_s, layer + 1)
                dve.scalar_tensor_tensor(gate, half_sign, 2.0, g, ALU.mult, ALU.mult)\
                   .then_inc(gate_a, 1)
                dve.wait_ge(gate_a, layer + 1)
                dve.scalar_tensor_tensor(gate, gate, GATE_MIN, half_sign, ALU.max, ALU.mult)\
                   .then_inc(gate_m, 1)
                if layer == 1:
                    dve.wait_ge(gate_m, 2)
                    dve.wait_ge(d_small, 48)
                    dve.tensor_tensor(gate, gate, adc[:, :].unsqueeze(2).to_broadcast([P, KT, NB]),
                                      ALU.mult).then_inc(gcol_ok, 1)

            def gate_linear(b, t):
                n = b * TT + t
                dve.wait_ge(att_done, n + 1)
                dve.wait_ge(gate_ok, b + 1)
                dve.wait_ge(xt_done, TT * NB + TT * b)
                if b:
                    dve.wait_ge(x1_ok, TT)
                dve.scalar_tensor_tensor(xn[:, t, :], bank[4 * b + t][:, :], 2.0, gates[:, b, :],
                                         ALU.mult, ALU.mult).then_inc(att_read, 1)

            def flag_vector(g):
                a, z = GROUPS[g]
                dve.wait_ge(checked, z)
                dve.tensor_reduce(flagv[:, g:g + 1], chk[:, a:z], AX_X, ALU.max)\
                   .then_inc(flagv_ok, 1)

            def read_flag(g):
                dve.wait_ge(flag_done, g + 1)
                dve.tensor_scalar(flags[0:1, g:g + 1], bank[3][0:1, 0:1], 0.0, None, ALU.is_gt)\
                   .then_inc(flag_ok, 1)

            def ffn_inner(s):
                c = s % C
                if s == 0:
                    dve.wait_ge(d_small, 48)
                dve.wait_ge(up_mm, s + 1)
                dve.wait_ge(silu_ok, s + 1)
                if s >= 2:
                    dve.wait_ge(in_lo, s - 1)
                dve.scalar_tensor_tensor(inner[:, s % 2, :], bank[gu_bank(s, 1)][:, :],
                                         scal[:, c, 1:2], silu_g[:, s % 2, :],
                                         ALU.mult, ALU.mult).then_inc(inner_ok, 1)
                dve.wait_ge(inner_ok, s + 1)
                if s >= 3:
                    wait_down(dve, s - 3)
                hi, lo = wsplit[:, 2 * (s % 3), :], wsplit[:, 2 * (s % 3) + 1, :]
                dve.tensor_copy(hi, inner[:, s % 2, :]).then_inc(in_hi, 1)
                dve.wait_ge(in_hi, s + 1)
                dve.tensor_tensor(lo, inner[:, s % 2, :], hi.bitcast(F32), ALU.subtract)\
                   .then_inc(in_lo, 1)

            def gate_ffn(b, t):
                n = b * TT + t
                dve.wait_ge(acc_mm, n + 1)
                dve.wait_ge(gate_ok, NB + b + 1)
                dve.wait_ge(xt_done, 4 * TT)
                if b:
                    dve.wait_ge(out_ok, TT)
                dve.scalar_tensor_tensor(xn[:, t, :], bank[4 + t][:, :], 2.0, gates[:, 2 + b, :],
                                         ALU.mult, ALU.mult).then_inc(acc_read, 1)

            for t in range(TT):
                stats(0, t)
            sum_mask(0)
            keep_blocks(0)
            normalise(0)
            mod_columns(0)
            sum_mask(1)
            keep_blocks(1)
            sum_mask(2)
            split(0)
            mod_columns(1)
            keep_blocks(2)
            split(1)
            stats(1, 0)
            sum_mask(3)
            mod_columns(2)
            keep_blocks(3)
            stats(1, 1)
            split(2)
            mod_columns(3)
            stats(1, 2)
            stats(1, 3)
            split(3)
            normalise(1)
            split(4)
            guard_gate(0, bank[7])
            split(5)
            split(6)
            gate_linear(0, 0)
            gate_linear(0, 1)
            split(7)
            gate_linear(0, 2)
            gate_linear(0, 3)
            for t in range(TT):
                stats(2, t)
            mod_columns(4)
            flag_vector(0)
            normalise(2)
            mod_columns(5)
            read_flag(0)
            for n in range(8, 12):
                split(n)
            for s in range(STEPS):
                if s == 0:
                    for t in range(TT):
                        gate_linear(1, t)
                if s == 2:
                    read_flag(1)
                if s == 5:
                    read_flag(2)
                ffn_inner(s)
                if s == 0:
                    stats(3, 0)
                    stats(3, 1)
                if s == 1:
                    stats(3, 2)
                    stats(3, 3)
                    flag_vector(1)
                if s == 2:
                    normalise(3)
                if s == 4:
                    flag_vector(2)
                    guard_gate(1, bank[3])
                if 6 <= s < 10:
                    split(6 + s)
                if s == C + LAG - 1:
                    for t in range(TT):
                        gate_ffn(0, t)
            for t in range(TT):
                n = TT + t
                gate_ffn(1, t)
                dve.wait_ge(acc_read, n + 1)
                dve.tensor_tensor(xt[:, n, :], xt[:, n, :], xn[:, t, :], ALU.add).then_inc(out_ok, 1)

        @block.tensor
        def _(pe):
            def mod_rows(n, w, src, dst):
                if n == 0:
                    pe.wait_ge(silu_c, 1)
                for j in range(KT):
                    last = pe.matmul(dst[32 * j:32 * (j + 1), 0:w], sc[:, j, :], src(j), start=True, stop=True)
                last.then_inc(rows_done, 1)

            def rows_ln1(k):
                pe.wait_ge(d_ln1[k], 16)
                if k:
                    pe.wait_ge(rows_copied, k)
                m = modw[:, k // 2, 2 * (k % 2):2 * (k % 2) + 2, :].rearrange("p a n -> p (a n)")
                mod_rows(k, D // 2, lambda j: m[:, j * (D // 2):(j + 1) * (D // 2)], bank[6])

            def columns(slot, count, dst):
                pe.wait_ge(sel_ok, 1)
                for i in range(count):
                    last = pe.matmul(dst[:, NB * i:NB * (i + 1)], rows[:, slot, i * P:(i + 1) * P],
                                     sel[:, :], start=True, stop=True)
                last.then_inc(cols_done, 1)

            def columns_ln1(k):
                pe.wait_ge(rows_copied, k + 1)
                pe.wait_ge(keep_ok, k + 1)
                columns(k % 2, 2, bank[7])

            def mask_blocks(k):
                pe.wait_ge(msum_ok, k + 1)
                pe.wait_ge(consts_ok, 6)
                if k:
                    pe.wait_ge(modc_ok, k)
                pe.matmul(bank[7][:, 0:NBLK], blkones[:, :], msum[:, k, :], start=True, stop=True)\
                  .then_inc(blk_done, 1)

            def transposes(n):
                q, k = divmod(n, KT)
                dst = bank[4 + n % 2] if q < 2 else bank[n % 2] if q == 2 else bank[3]
                if k == 0:
                    pe.wait_ge(xn_ok, TT * (q + 1))
                if q == 2 and k < 2:
                    pe.wait_ge(att_read, k + 1)
                elif q == 3:
                    pe.wait_ge(h_ok, n)
                elif n >= 2:
                    pe.wait_ge(h_ok, n - 1)
                for t in range(TT):
                    last = pe.transpose(dst[:, t * P:(t + 1) * P], xn[:, t, k * P:(k + 1) * P],
                                        ident[:, :])
                last.then_inc(xt_done, 1)

            def linear_part(b, k, t, part):
                for wpart in range(2):
                    if b == 0 and t == 0 and part == 0:
                        pe.wait_ge(w_lo if wpart else w_hi, k + 1)
                    last = pe.matmul(bank[4 * b + t][:, :],
                                     ht[:, b, k, part, t * P:(t + 1) * P],
                                     wsplit[:, 2 * k + wpart, :],
                                     start=(k == 0 and part == 0 and wpart == 0),
                                     stop=(k == KT - 1 and part == 1 and wpart == 1))
                return last

            def linear(b, k, t):
                if t == 0:
                    wait_split(pe, TT * b + k)
                if b == 1 and k == 0:
                    if t < 2:
                        pe.wait_ge(h_ok, 7 + t)
                    else:
                        pe.wait_ge(gate_ok, t - 1)
                linear_part(b, k, t, 0)
                last = linear_part(b, k, t, 1)
                if k == KT - 1:
                    last.then_inc(att_done, 1)

            def gate_all(layer, b, dst):
                for k in range(KT):
                    last = pe.matmul(dst[:, k * P:(k + 1) * P],
                                     gcol[:, layer, k, b:b + 1].to_broadcast([P, P]), ident[:, :],
                                     start=True, stop=True)
                last.then_inc(gate_done, 1)

            def flag_sum(g):
                pe.wait_ge(flagv_ok, g + 1)
                pe.matmul(bank[3][0:1, 0:1], flagv[:, g:g + 1], onecol[:, :], start=True, stop=True)\
                  .then_inc(flag_done, 1)

            general = []

            def load_flag(g):
                pe.wait_ge(flag_ok, g + 1)
                general.append(pe.value_load(flags[0:1, g:g + 1], min_val=0, max_val=1))

            def gate_up_product(s, u, k, part, native):
                b, c = divmod(s, C)
                w = whi_gu[:, s % 2, (u * KT + k) * P:(u * KT + k + 1) * P]
                h = ht[:, b, k, part, :]
                if native:
                    w, h = raw_gu(c, u, k), h.bitcast(F32)
                return pe.matmul(bank[gu_bank(s, u)][:, :], w, h, start=(k == 0 and part == 0),
                                 stop=(k == KT - 1 and part == 1))

            def gate_up_first():
                pe.wait_ge(wgu_hi, 1)
                pe.wait_ge(modc_ok, KT + 2)
                pe.wait_ge(h_ok, 11)

                def products(native):
                    for k in range(KT):
                        for part in range(2):
                            pe.wait_ge((h_lo if part else h_hi)[2], k + 1)
                            for u in range(2):
                                last = gate_up_product(0, u, k, part, native)
                                if k == KT - 1 and part == 1:
                                    last.then_inc(up_mm if u else gate_mm, 1)

                with pe.If(general[0]):
                    products(True)
                with pe.Else():
                    products(False)

            def gate_up(s):
                b, c = divmod(s, C)
                pe.wait_ge(wgu_hi, s + 1)

                def products(u, native, done):
                    for k in range(KT):
                        if c == 0 and u == 0:
                            wait_split(pe, TT * (2 + b) + k)
                        for part in range(2):
                            last = gate_up_product(s, u, k, part, native)
                    last.then_inc(done, 1)

                if s == 1:
                    pe.wait_ge(h_ok, 12)
                else:
                    pe.wait_ge(inner_ok, s - 1)
                yes = general[GROUP_OF[c]]
                with pe.If(yes):
                    products(0, True, gate_mm)
                with pe.Else():
                    products(0, False, gate_mm)
                pe.wait_ge(silu_ok, s)
                with pe.If(yes):
                    products(1, True, up_mm)
                with pe.Else():
                    products(1, False, up_mm)

            def down(s):
                b, c = divmod(s, C)
                pe.wait_ge(in_lo, s + 1)
                pe.wait_ge(wd_hi, s + 1)

                def products(t, native):
                    for part in range(2):
                        h = wsplit[:, 2 * (s % 3) + part, t * P:(t + 1) * P]
                        w = whi_d(s)
                        if native:
                            h, w = h.bitcast(F32), raw_d(c)
                        last = pe.matmul(bank[4 + t][:, :], h, w, start=(c == 0 and part == 0),
                                         stop=(c == C - 1 and part == 1))
                    if c == C - 1:
                        last.then_inc(acc_mm, 1)
                    elif t == TT - 1:
                        last.then_inc(down_mm, 1)

                if c == 0:
                    if b == 0:
                        pe.wait_ge(att_read, 2 * TT)
                    else:
                        pe.wait_ge(acc_read, TT)
                with pe.If(general[GROUP_OF[c]]):
                    for t in range(TT):
                        products(t, True)
                with pe.Else():
                    for t in range(TT):
                        products(t, False)

            def gate_rows():
                pe.wait_ge(d_gate[0], 16)
                pe.wait_ge(rows_copied, KT)
                mod_rows(4, D, lambda j: modw[:, 2, j, :], bank[6])

            def gate_columns():
                pe.wait_ge(rows_copied, KT + 1)
                pe.wait_ge(modc_ok, KT)
                columns(2, KT, bank[7])

            def gate_first(b):
                pe.wait_ge(gate_m, 1)
                gate_all(0, b, bank[6 + b])

            pe.wait_ge(ident_ok, 1)
            for _ in range(WARM_UP):
                pe.matmul(bank[0][:, 0:P], ident[:, :], ident[:, :], start=True, stop=True)
            mask_blocks(0)
            rows_ln1(0)
            columns_ln1(0)
            transposes(0)
            transposes(1)
            mask_blocks(1)
            rows_ln1(1)
            columns_ln1(1)
            between = {
                (0, 1): [lambda: rows_ln1(2)],
                (0, 2): [lambda: transposes(2)],
                (0, 3): [lambda: columns_ln1(2)],
                (1, 0): [lambda: mask_blocks(3)],
                (1, 1): [lambda: rows_ln1(3)],
                (1, 2): [lambda: transposes(3)],
                (1, 3): [lambda: columns_ln1(3)],
                (3, 0): [gate_rows, lambda: transposes(4)],
                (3, 1): [lambda: transposes(5), gate_columns],
                (3, 2): [lambda: gate_first(0)],
                (3, 3): [lambda: gate_first(1), lambda: transposes(6), lambda: transposes(7)],
            }
            for k in range(KT):
                if k == 0:
                    pe.wait_ge(h_hi[0], 1)
                    for t in range(TT):
                        linear_part(0, 0, t, 0)
                    mask_blocks(2)
                for t in range(TT):
                    if k:
                        linear(0, k, t)
                    else:
                        wait_split(pe, 0)
                        linear_part(0, 0, t, 1)
                    for more in between.get((k, t), []):
                        more()
            for k in range(KT):
                for t in range(TT):
                    linear(1, k, t)
                    if (k, t) == (0, 3):
                        pe.wait_ge(d_ln2[0], 16)
                        pe.wait_ge(att_read, 3)
                        mod_rows(5, D, lambda j: modw[:, 0, j, :], bank[2])
                    if (k, t) == (1, 1):
                        pe.wait_ge(rows_copied, 6)
                        pe.wait_ge(att_read, 4)
                        columns(0, KT, bank[3])
                        pe.wait_ge(d_ln2[1], 16)
                        mod_rows(6, D, lambda j: modw[:, 1, j, :], bank[2])
                    if (k, t) == (1, 3):
                        pe.wait_ge(rows_copied, 7)
                        columns(1, KT, bank[2])
                    if (k, t) == (2, 2):
                        pe.wait_ge(modc_ok, KT + 1)
                        flag_sum(0)
                    if (k, t) == (2, 3):
                        transposes(8)
                        transposes(9)
                    if (k, t) == (3, 1):
                        transposes(10)
                    if (k, t) == (3, 2):
                        transposes(11)
            load_flag(0)
            for s in range(STEPS + LAG):
                if s == GROUPS[1][0]:
                    load_flag(1)
                if s == GROUPS[2][0]:
                    load_flag(2)
                if s == 0:
                    gate_up_first()
                elif s < STEPS:
                    gate_up(s)
                if s == 2:
                    flag_sum(1)
                if s == 5:
                    pe.wait_ge(gcol_ok, 1)
                    flag_sum(2)
                if s >= LAG:
                    down(s - LAG)
                if s == 3:
                    pe.wait_ge(d_gate[1], 16)
                    mod_rows(7, D, lambda j: modw[:, 2, j, :], bank[3])
                if s == 4:
                    pe.wait_ge(rows_copied, 8)
                    columns(2, KT, bank[3])
                if 6 <= s < 10:
                    transposes(6 + s)
                if s == 10:
                    pe.wait_ge(h_ok, 4 * TT)
                    gate_all(1, 0, bank[3])
                if s == 11:
                    pe.wait_ge(gate_ok, 3)
                    gate_all(1, 1, bank[3])


def kernel(L0_attn_data, L0_attn_weight, L0_attn_mask, L0_ffn_Wg, L0_ffn_Wu, L0_ffn_Wd, L0_ffn_ag,
           L0_ffn_au, L0_ffn_ad, L0_c, L0_wmod):
    import numpy as np
    from concourse import bacc
    from concourse.bass_utils import run_bass_kernel_spmd

    def c_(a):
        return np.ascontiguousarray(a)

    x = np.asarray(L0_attn_data)
    shape = x.shape
    nf = C - 1
    wmod = np.asarray(L0_wmod).reshape(KT, P, 6, D)

    def ln_weights(scale, shift):
        w = wmod[:, :, [scale, shift], :].reshape(KT, P, 2, KT, P)
        return w.transpose(3, 1, 0, 2, 4)

    gu = np.stack([np.asarray(L0_ffn_Wg), np.asarray(L0_ffn_Wu)])
    gu_full = gu[:, :nf * P].reshape(2, nf, P, KT, P).transpose(1, 4, 0, 3, 2)
    gu_tail = gu[:, nf * P:].reshape(2, FT, KT, P).transpose(3, 0, 2, 1)
    sc = np.stack([np.asarray(L0_ffn_ag), np.asarray(L0_ffn_au)])
    ln2 = ln_weights(4, 3).reshape(2, 2, P, KT, 2 * P).transpose(0, 2, 3, 1, 4)
    arrays = {
        "x": c_(x.reshape(NB * SEQ, D)),
        "att_w": c_(np.asarray(L0_attn_weight).T),
        "att_mask": c_(np.asarray(L0_attn_mask).T),
        "cond": c_(np.asarray(L0_c).T.reshape(KT, P, NB).transpose(1, 0, 2)),
        "mod_ln1": c_(ln_weights(1, 0).reshape(KT, P, 2, D)),
        "mod_ln2": c_(ln2.reshape(2, P, KT, D)),
        "mod_gate": c_(wmod[:, :, [2, 5], :].transpose(2, 1, 0, 3)),
        "w_gu": c_(gu_full.reshape(nf, P, 2 * D)),
        "w_gu_tail": c_(gu_tail.reshape(P, 2 * KT, FT)),
        "w_down": c_(np.asarray(L0_ffn_Wd).T),
        "scales": c_(sc[:, :nf * P].reshape(2, nf, P).transpose(2, 1, 0)),
        "scales_tail": c_(sc[:, nf * P:].T),
        "down_scale": c_(np.asarray(L0_ffn_ad).reshape(KT, P).T),
    }
    nc = bacc.Bacc("TRN2", target_bir_lowering=False, num_devices=1)
    args = [nc.dram_tensor(f"in_{name}", a.shape, mybir.dt.from_np(a.dtype), kind="ExternalInput").ap()
            for name, a in arrays.items()]
    args.append(nc.dram_tensor("out_0", (NB * SEQ, D), F32, kind="ExternalOutput").ap())
    adaln_block(nc, *args)
    r = run_bass_kernel_spmd(nc, [{f"in_{name}": a for name, a in arrays.items()}], core_ids=[0])
    return r.results[0]["out_0"].reshape(shape)
```

```python
from contextlib import ExitStack

import concourse.bass as bass
from concourse import mybir

F32 = mybir.dt.float32
F32R = mybir.dt.float32r
I32 = mybir.dt.int32
U16 = mybir.dt.uint16
U8 = mybir.dt.uint8
ALU = mybir.AluOpType
ACT = mybir.ActivationFunctionType
AX_X = mybir.AxisListType.X

P = 128
D = 512
KT = D // P
NB = 2
TT = 4
SEQ = TT * P
F = 1376
C = -(-F // P)
FT = F - (C - 1) * P
BLK = 32
NBLK = D // BLK
EPS = 1e-5
GATE_MIN = 0.25
STEPS = NB * C
WARM_UP = 18
BY_POOL = 6
H1_CHUNK = C + -NB * KT * SEQ // (3 * D)
LAG = 2
CHECKS_AT = {0: 3, 2: 1, 3: 2}
GROUPS = [(0, 5), (5, C)]
GROUP_OF = [g for g, (a, b) in enumerate(GROUPS) for _ in range(a, b)]


def gu_bank(s, u):
    return 3 if (s, u) == (1, 1) else (2 * s + u + 2) % 3


def adaln_block(nc, x, att_w, att_mask, cond, mod_ln1, mod_ln2, mod_gate, w_gu, w_gu_tail, w_down,
                scales, scales_tail, down_scale, out):
    with ExitStack() as ctx:
        def sb(name, shape, dt=F32):
            return ctx.enter_context(nc.sbuf_tensor(name, shape, dt))

        def sem(name):
            return ctx.enter_context(nc.semaphore(name))

        xt = sb("xt", [P, NB * TT, D])
        xn = sb("xn", [P, TT, D])
        ht = sb("ht", [P, NB, KT, 2, SEQ], F32R)
        hbuf = sb("hbuf", [P, 2, SEQ])
        awork = sb("awork", [P, KT, D])
        maskt = sb("maskt", [P, KT, D], I32)
        in_split = sb("in_split", [P, 3, 2, D], F32R)
        modw = sb("modw", [P, 3, KT, D])
        rows = sb("rows", [P, 3, D])
        wffn = sb("wffn", [P, C, 3 * D])
        whi_gu = sb("whi_gu", [P, 2, 2 * D], F32R)
        whi_dn = sb("whi_dn", [P, 3, D], F32R)
        junk = sb("junk", [P, 3 * D], U8)
        scal = sb("scal", [P, C, 2])
        adc = sb("adc", [P, KT])
        gcol = sb("gcol", [P, 2, KT, NB])
        gscr = sb("gscr", [P, 2, KT, NB])
        condt = sb("condt", [P, KT, NB])
        sc = sb("sc", [P, KT, BLK])
        ident = sb("ident", [P, P])
        blkones = sb("blkones", [P, P])
        oneplus = sb("oneplus", [P, 8])
        onecol = sb("onecol", [P, 1])
        msum = sb("msum", [P, KT, NBLK])
        keep = sb("keep", [P, KT, NBLK])
        colv = sb("colv", [P, 8, KT, NB])
        modc = sb("modc", [P, 2, KT, 4])
        bns = sb("bns", [P, 2 * NB, TT, 6])
        mv = sb("mv", [P, 2 * NB, TT, 2])
        veps = sb("veps", [P, 2 * NB, TT])
        rstd = sb("rstd", [P, 2 * NB, TT])
        mhalf = sb("mhalf", [P, TT])
        chk = sb("chk", [P, C])
        flagv = sb("flagv", [P, len(GROUPS)])
        flags = sb("flags", [1, len(GROUPS)], I32)

        gates = maskt[:, :, :].bitcast(F32)
        h1 = wffn[:, H1_CHUNK:C, :].rearrange("p c n -> p (c n)")[:, 0:NB * KT * SEQ]\
            .rearrange("p (b k t) -> p b k t", b=NB, k=KT)
        silu_g = awork[:, 0:2, :]
        inner = awork[:, 2:4, :]

        def raw_gu(c, u, k):
            return wffn[:, c, (u * KT + k) * P:(u * KT + k + 1) * P]

        def raw_d(c):
            return wffn[:, c, 2 * D:3 * D]

        def whi_d(s):
            return whi_dn[:, s % 3, :]

        bank = [ctx.enter_context(nc.psum_tensor(f"bank{i}", [P, D], F32)) for i in range(8)]

        d_cond = sem("d_cond")
        d_x = [sem(f"d_x{t}") for t in range(NB * TT)]
        d_ln1 = [sem(f"d_ln1_{k}") for k in range(KT)]
        d_att = [sem(f"d_att{k}") for k in range(KT)]
        d_mask = [sem(f"d_mask{k}") for k in range(KT)]
        d_ln2 = [sem(f"d_ln2_{k}") for k in range(2)]
        d_gate = [sem(f"d_gate{k}") for k in range(2)]
        d_ffn = [sem(f"d_ffn{c}") for c in range(C)]
        d_small = sem("d_small")
        d_out = sem("d_out")
        zeroed = sem("zeroed")
        tail_zero = sem("tail_zero")
        ident_z = sem("ident_z")
        ident_ok = sem("ident_ok")
        consts_ok = sem("consts_ok")
        silu_c = sem("silu_c")
        rows_done = sem("rows_done")
        rows_copied = sem("rows_copied")
        cols_done = sem("cols_done")
        cols_ok = sem("cols_ok")
        modc_ok = sem("modc_ok")
        gate_s = sem("gate_s")
        gate_a = sem("gate_a")
        gate_m = sem("gate_m")
        gcol_ok = sem("gcol_ok")
        gate_done = sem("gate_done")
        gate_ok = sem("gate_ok")
        msum_ok = sem("msum_ok")
        blk_done = sem("blk_done")
        keep_ok = sem("keep_ok")
        masked = sem("masked")
        bn_done = sem("bn_done")
        stats_ok = sem("stats_ok")
        veps_ok = sem("veps_ok")
        rstd_ok = sem("rstd_ok")
        xn_ok = sem("xn_ok")
        xt_done = sem("xt_done")
        h_ok = sem("h_ok")
        h_hi = sem("h_hi")
        h_lo = sem("h_lo")
        att_done = sem("att_done")
        att_read = sem("att_read")
        x1_ok = sem("x1_ok")
        checked = sem("checked")
        flagv_ok = sem("flagv_ok")
        flag_done = sem("flag_done")
        flag_ok = sem("flag_ok")
        wgu_hi = sem("wgu_hi")
        wd_hi = sem("wd_hi")
        gate_mm = sem("gate_mm")
        up_mm = sem("up_mm")
        silu_ok = sem("silu_ok")
        inner_ok = sem("inner_ok")
        in_hi = sem("in_hi")
        in_lo = sem("in_lo")
        down_mm = sem("down_mm")
        acc_mm = sem("acc_mm")
        acc_read = sem("acc_read")
        out_ok = sem("out_ok")
        out_last = sem("out_last")

        def wait_down(eng, s):
            if s % C == C - 1:
                eng.wait_ge(acc_mm, TT * (s // C + 1))
            else:
                eng.wait_ge(down_mm, s - s // C + 1)

        block = ctx.enter_context(nc.Block())

        @block.sync
        def _(sp):
            for t in range(TT):
                sp.dma_start(xt[:, t, :], x[t * P:(t + 1) * P, :]).then_inc(d_x[t], 16)

            def load_att(k):
                sp.dma_start(maskt[:, k, :], att_mask[k * P:(k + 1) * P, :]).then_inc(d_mask[k], 16)
                sp.dma_start(modw[:, k // 2, 2 * (k % 2):2 * (k % 2) + 2, :], mod_ln1[k])\
                  .then_inc(d_ln1[k], 16)
                sp.dma_start(awork[:, k, :], att_w[k * P:(k + 1) * P, :]).then_inc(d_att[k], 16)

            def load_x(t):
                sp.dma_start(xt[:, t, :], x[t * P:(t + 1) * P, :]).then_inc(d_x[t], 16)

            for k in range(KT):
                load_att(k)
            for t in range(TT, NB * TT):
                load_x(t)
            sp.dma_start(modw[:, 2, :, :], mod_gate[0]).then_inc(d_gate[0], 16)
            sp.wait_ge(rows_done, 2)
            sp.dma_start(modw[:, 0, :, :], mod_ln2[0]).then_inc(d_ln2[0], 16)
            for c in range(C):
                if c == H1_CHUNK:
                    sp.wait_ge(att_done, NB * TT)
                if c == 1:
                    sp.wait_ge(rows_done, 4)
                    sp.dma_start(modw[:, 1, :, :], mod_ln2[1]).then_inc(d_ln2[1], 16)
                if c < C - 1:
                    sp.dma_start(wffn[:, c, 0:2 * D], w_gu[c]).then_inc(d_ffn[c], 16)
                    sp.dma_start(raw_d(c), w_down[c * P:(c + 1) * P, :]).then_inc(d_ffn[c], 16)
                else:
                    sp.wait_ge(tail_zero, 1)
                    sp.dma_start(wffn[:, c, 0:2 * D].rearrange("p (n i) -> p n i", i=P)[:, :, 0:FT],
                                 w_gu_tail).then_inc(d_ffn[c], 16)
                    sp.dma_start(wffn[0:FT, c, 2 * D:3 * D], w_down[c * P:F, :])\
                      .then_inc(d_ffn[c], 16)
                if c == 4:
                    sp.wait_ge(rows_done, KT + 1)
                    sp.dma_start(modw[:, 2, :, :], mod_gate[1]).then_inc(d_gate[1], 16)
            for n in range(BY_POOL):
                sp.wait_ge(out_ok, n + 1)
                sp.dma_start(out[n * P:(n + 1) * P, :], xt[:, n, :]).then_inc(d_out, 16)
            sp.wait_ge(d_out, 16 * NB * TT)

        @block.gpsimd
        def _(pool):
            pool.memset(ident[:, :], 0.0).then_inc(ident_z, 1)
            pool.memset(mhalf[:, :], -0.5).then_inc(ident_z, 1)
            pool.wait_ge(ident_z, 2)
            pool.affine_select(out=ident[:, :], in_=ident[:, :], compare_op=ALU.not_equal, fill=1.0,
                               base=0, pattern=[[-1, P]], channel_multiplier=1).then_inc(ident_ok, 1)

            def inverse_deviation(q, half):
                two = slice(2 * half, 2 * half + 2)
                pool.wait_ge(stats_ok, TT * q + 2 * half + 2)
                pool.tensor_scalar(veps[:, q, two], mv[:, q, two, 1], EPS, None, ALU.add)\
                    .then_inc(veps_ok, 1)
                pool.wait_ge(veps_ok, 2 * q + half + 1)
                pool.tensor_tensor(rstd[:, q, two], veps[:, q, two], mhalf[:, 0:2], ALU.pow)\
                    .then_inc(rstd_ok, 1)

            def mask_weights(k):
                pool.wait_ge(d_att[k], 16)
                pool.wait_ge(keep_ok, k + 1)
                w = awork[:, k, :].rearrange("p (b i) -> p b i", i=BLK)
                pool.tensor_tensor(w, w, keep[:, k, :].unsqueeze(2).to_broadcast([P, NBLK, BLK]),
                                   ALU.mult).then_inc(masked, 1)

            def add_to_x(b, t):
                n = b * TT + t
                pool.wait_ge(att_read, n + 1)
                pool.tensor_tensor(xt[:, n, :], xt[:, n, :], xn[:, t, :], ALU.add).then_inc(x1_ok, 1)

            inverse_deviation(0, 0)
            inverse_deviation(0, 1)
            for k in range(KT):
                mask_weights(k)
            inverse_deviation(1, 0)
            inverse_deviation(1, 1)
            for b in range(NB):
                for t in range(TT):
                    add_to_x(b, t)
                inverse_deviation(2 + b, 0)
                inverse_deviation(2 + b, 1)
                if b == 0:
                    pool.wait_ge(att_done, NB * TT)
                    pool.memset(wffn[:, C - 1, :], 0.0).then_inc(tail_zero, 1)
            for n in range(BY_POOL):
                pool.wait_ge(acc_read, n + 1)
                pool.tensor_tensor(xt[:, n, :], xt[:, n, :], xn[:, n % TT, :], ALU.add)\
                    .then_inc(out_ok, 1)

        @block.scalar
        def _(act):
            act.dma_start(condt[:, :, :], cond).then_inc(d_cond, 16)
            act.dma_start(scal[:, 0:C - 1, :], scales).then_inc(d_small, 16)
            act.dma_start(adc[:, :], down_scale).then_inc(d_small, 16)
            act.wait_ge(zeroed, 2)
            act.dma_start(scal[0:FT, C - 1, :], scales_tail).then_inc(d_small, 16)
            act.wait_ge(d_cond, 16)
            act.wait_ge(zeroed, 3)
            act.activation(sc[:, :, 0:NB], condt[:, :, :], ACT.Silu).then_inc(silu_c, 1)

            ROWS_BANK = [6, 6, 6, 6, 6, 2, 2, 3]
            ROWS_SLOT = [0, 1, 0, 1, 2, 0, 1, 2]
            ROWS_LAST = {2: 0, 3: 1, 5: 2, 6: 3, 7: 4}

            def copy_rows(n):
                w = D // 2 if n < KT else D
                act.wait_ge(rows_done, n + 1)
                if n in ROWS_LAST:
                    act.wait_ge(cols_done, ROWS_LAST[n] + 1)
                act.activation(rows[:, ROWS_SLOT[n], 0:w], bank[ROWS_BANK[n]][:, 0:w], ACT.Copy)\
                   .then_inc(rows_copied, 1)

            def copy_gate(n, src):
                act.wait_ge(gate_done, n + 1)
                act.wait_ge(msum_ok, KT)
                act.activation(gates[:, n, :], src[:, :], ACT.Copy).then_inc(gate_ok, 1)

            def modulate(n):
                q, k = divmod(n, KT)
                layer, b = divmod(q, NB)
                act.wait_ge(xt_done, n + 1)
                act.wait_ge(modc_ok, k + 1 if layer == 0 else KT + 1 + k // 2)
                if q < 2:
                    dst = h1[:, b, k, :]
                else:
                    dst = hbuf[:, n % 2, :]
                    if n >= 10:
                        act.wait_ge(h_lo, n - 9)
                src = bank[4 + n % 2] if q < 2 else bank[n % 2] if q == 2 else bank[3]
                act.activation(dst, src[:, :], ACT.Identity,
                               bias=modc[:, layer, k, 2 + b:3 + b],
                               scale=modc[:, layer, k, b:b + 1]).then_inc(h_ok, 1)

            def check_chunk(c):
                act.wait_ge(d_ffn[c], 32)
                if c == C - 1:
                    act.wait_ge(tail_zero, 1)
                if c:
                    act.wait_ge(checked, c)
                low = wffn[:, c, :].bitcast(U16).rearrange("p (n h) -> p n h", h=2)[:, :, 0]
                act.activation(junk[:, :], low, ACT.Copy, accum_out=chk[:, c:c + 1])\
                   .then_inc(checked, 1)

            def round_gu(s):
                act.wait_ge(d_ffn[s % C], 32)
                if s >= 2:
                    act.wait_ge(up_mm, s - 1)
                act.activation(whi_gu[:, s % 2, :], wffn[:, s % C, 0:2 * D], ACT.Copy)\
                   .then_inc(wgu_hi, 1)

            def round_d(s):
                if s >= 3:
                    wait_down(act, s - 3)
                act.activation(whi_d(s), raw_d(s % C), ACT.Copy).then_inc(wd_hi, 1)

            for k in range(KT):
                copy_rows(k)
                modulate(k)
            check_at = iter(range(C))
            copy_rows(4)
            modulate(4)
            modulate(5)
            copy_gate(0, bank[6])
            modulate(6)
            modulate(7)
            copy_gate(1, bank[7])
            check_chunk(next(check_at))
            copy_rows(5)
            check_chunk(next(check_at))
            copy_rows(6)
            for _ in range(3):
                check_chunk(next(check_at))
            round_gu(0)
            for n in range(8, 12):
                modulate(n)
            for s in range(STEPS):
                if s + 1 < STEPS:
                    round_gu(s + 1)
                if s == 0:
                    for _ in range(CHECKS_AT[s]):
                        check_chunk(next(check_at))
                act.wait_ge(gate_mm, s + 1)
                if s == 0:
                    act.wait_ge(d_small, 48)
                if s >= 2:
                    act.wait_ge(inner_ok, s - 1)
                act.activation(silu_g[:, s % 2, :], bank[gu_bank(s, 0)][:, :], ACT.Silu,
                               scale=scal[:, s % C, 0:1]).then_inc(silu_ok, 1)
                round_d(s)
                if s > 0:
                    for _ in range(CHECKS_AT.get(s, 0)):
                        check_chunk(next(check_at))
                if s == 2:
                    copy_rows(7)
                if s == 10:
                    copy_gate(2, bank[3])
                if s == 11:
                    copy_gate(3, bank[3])
                if 6 <= s < 10:
                    modulate(6 + s)
            for n in range(BY_POOL, NB * TT):
                act.wait_ge(out_last, n - BY_POOL + 1)
                act.dma_start(out[n * P:(n + 1) * P, :], xt[:, n, :]).then_inc(d_out, 16)

        @block.vector
        def _(dve):
            dve.memset(blkones[:, :], 0.0).then_inc(zeroed, 1)
            dve.memset(scal[:, C - 1, :], 0.0).then_inc(zeroed, 1)
            dve.memset(sc[:, :, :], 0.0).then_inc(zeroed, 1)
            dve.memset(oneplus[:, :], 0.0).then_inc(zeroed, 1)
            dve.wait_ge(zeroed, 4)
            for g in range(P // BLK):
                s = slice(g * BLK, (g + 1) * BLK)
                dve.memset(blkones[s, s], 1.0).then_inc(consts_ok, 1)
            dve.memset(onecol[:, :], 1.0).then_inc(consts_ok, 1)
            ones = oneplus[:, :].rearrange("p (g v b) -> p g v b", g=2, v=2)[:, :, 0, :]
            dve.memset(ones, 1.0).then_inc(consts_ok, 1)
            def stats(q, t):
                n = q * TT + t
                if q < 2:
                    dve.wait_ge(d_x[n], 16)
                else:
                    dve.wait_ge(x1_ok, n - NB * TT + 1)
                dve.bn_stats(bns[:, q, t, :], xt[:, n % (NB * TT), :]).then_inc(bn_done, 1)
                dve.wait_ge(bn_done, n + 1)
                dve.bn_aggr(mv[:, q, t, :], bns[:, q, t, :]).then_inc(stats_ok, 1)

            def normalise(q, tiles=range(TT)):
                if q:
                    dve.wait_ge(xt_done, TT * q)
                if q >= 2:
                    dve.wait_ge(x1_ok, TT * (q - 1))
                for t in tiles:
                    if t % 2 == 0:
                        dve.wait_ge(rstd_ok, 2 * q + t // 2 + 1)
                        dve.wait_ge(stats_ok, TT * q + t + 2)
                    dve.tensor_scalar(xn[:, t, :], xt[:, q % NB * TT + t, :], mv[:, q, t, 0:1],
                                      rstd[:, q, t:t + 1], ALU.subtract, ALU.mult).then_inc(xn_ok, 1)

            def sum_mask(k):
                dve.wait_ge(d_mask[k], 16)
                dve.tensor_reduce(msum[:, k, :], maskt[:, k, :].rearrange("p (b i) -> p b i", i=BLK),
                                  AX_X, ALU.add).then_inc(msum_ok, 1)

            def keep_blocks(k):
                dve.wait_ge(blk_done, k + 1)
                dve.tensor_scalar(keep[:, k, :], bank[7][:, 0:NBLK], 0.0, None, ALU.is_gt)\
                   .then_inc(keep_ok, 1)

            def sum_columns(use, count, src):
                dve.wait_ge(cols_done, use + 1)
                part = src[:, 0:count * P].rearrange("p (i j r) -> p i r j", j=KT, r=BLK)
                dve.tensor_reduce(colv[:, use, 0:count, :], part[:, :, 0:NB, :], AX_X, ALU.add)\
                   .then_inc(cols_ok, 1)
                dve.wait_ge(cols_ok, use + 1)

            def mod_columns(n):
                use = n if n < KT else n + 1
                count = 2 if n < KT else KT
                sum_columns(use, count, bank[7 if n < KT else 7 - n])
                dve.wait_ge(consts_ok, 6)
                dst = modc[:, 0, n, :] if n < KT else \
                    modc[:, 1, 2 * (n - KT):2 * (n - KT) + 2, :].rearrange("p k v -> p (k v)")
                dve.tensor_tensor(dst, colv[:, use, 0:count, :].rearrange("p i b -> p (i b)"),
                                  oneplus[:, 0:count * NB], ALU.add).then_inc(modc_ok, 1)

            def split(n):
                b, k = divmod(n - NB * KT, KT)
                i = n - NB * KT + 1
                dve.wait_ge(h_ok, n + 1)
                dve.tensor_copy(ht[:, b, k, 0, :], hbuf[:, n % 2, :]).then_inc(h_hi, 1)
                dve.wait_ge(h_hi, i)
                dve.tensor_tensor(ht[:, b, k, 1, :], hbuf[:, n % 2, :],
                                  ht[:, b, k, 0, :].bitcast(F32), ALU.subtract).then_inc(h_lo, 1)

            def guard_gate(layer, src):
                use = KT if layer == 0 else 2 * KT - 1
                sum_columns(use, KT, src)
                g = colv[:, use, :, :]
                half_sign, gate = gscr[:, layer, :, :], gcol[:, layer, :, :]
                dve.tensor_scalar(half_sign, g, 0.0, 0.5, ALU.is_ge, ALU.subtract)\
                   .then_inc(gate_s, 1)
                dve.wait_ge(gate_s, layer + 1)
                dve.scalar_tensor_tensor(gate, half_sign, 2.0, g, ALU.mult, ALU.mult)\
                   .then_inc(gate_a, 1)
                dve.wait_ge(gate_a, layer + 1)
                dve.scalar_tensor_tensor(gate, gate, GATE_MIN, half_sign, ALU.max, ALU.mult)\
                   .then_inc(gate_m, 1)
                if layer == 1:
                    dve.wait_ge(gate_m, 2)
                    dve.wait_ge(d_small, 48)
                    dve.tensor_tensor(gate, gate, adc[:, :].unsqueeze(2).to_broadcast([P, KT, NB]),
                                      ALU.mult).then_inc(gcol_ok, 1)

            def gate_linear(b, t):
                n = b * TT + t
                dve.wait_ge(att_done, n + 1)
                dve.wait_ge(gate_ok, b + 1)
                dve.wait_ge(xt_done, TT * NB + TT * b)
                if b:
                    dve.wait_ge(x1_ok, TT)
                dve.scalar_tensor_tensor(xn[:, t, :], bank[4 * b + t][:, :], 2.0, gates[:, b, :],
                                         ALU.mult, ALU.mult).then_inc(att_read, 1)

            def flag_vector(g):
                a, z = GROUPS[g]
                dve.wait_ge(checked, z)
                dve.tensor_reduce(flagv[:, g:g + 1], chk[:, a:z], AX_X, ALU.max)\
                   .then_inc(flagv_ok, 1)

            def read_flag(g):
                dve.wait_ge(flag_done, g + 1)
                dve.tensor_scalar(flags[0:1, g:g + 1], bank[3][0:1, 0:1], 0.0, None, ALU.is_gt)\
                   .then_inc(flag_ok, 1)

            def ffn_inner(s):
                c = s % C
                if s == 0:
                    dve.wait_ge(d_small, 48)
                dve.wait_ge(up_mm, s + 1)
                dve.wait_ge(silu_ok, s + 1)
                if s >= 2:
                    dve.wait_ge(in_lo, s - 1)
                dve.scalar_tensor_tensor(inner[:, s % 2, :], bank[gu_bank(s, 1)][:, :],
                                         scal[:, c, 1:2], silu_g[:, s % 2, :],
                                         ALU.mult, ALU.mult).then_inc(inner_ok, 1)
                dve.wait_ge(inner_ok, s + 1)
                if s >= 3:
                    wait_down(dve, s - 3)
                hi, lo = in_split[:, s % 3, 0, :], in_split[:, s % 3, 1, :]
                dve.tensor_copy(hi, inner[:, s % 2, :]).then_inc(in_hi, 1)
                dve.wait_ge(in_hi, s + 1)
                dve.tensor_tensor(lo, inner[:, s % 2, :], hi.bitcast(F32), ALU.subtract)\
                   .then_inc(in_lo, 1)

            def gate_ffn(b, t):
                n = b * TT + t
                dve.wait_ge(acc_mm, n + 1)
                dve.wait_ge(gate_ok, NB + b + 1)
                dve.wait_ge(xt_done, 4 * TT)
                if b:
                    dve.wait_ge(out_ok, TT)
                dve.scalar_tensor_tensor(xn[:, t, :], bank[4 + t][:, :], 2.0, gates[:, 2 + b, :],
                                         ALU.mult, ALU.mult).then_inc(acc_read, 1)

            for t in range(TT):
                stats(0, t)
            normalise(0, (0, 1))
            sum_mask(0)
            normalise(0, (2, 3))
            keep_blocks(0)
            mod_columns(0)
            sum_mask(1)
            keep_blocks(1)
            mod_columns(1)
            sum_mask(2)
            keep_blocks(2)
            sum_mask(3)
            mod_columns(2)
            keep_blocks(3)
            stats(1, 0)
            stats(1, 1)
            mod_columns(3)
            stats(1, 2)
            stats(1, 3)
            normalise(1)
            guard_gate(0, bank[7])
            for t in range(TT):
                gate_linear(0, t)
            for t in range(TT):
                stats(2, t)
            mod_columns(4)
            normalise(2)
            mod_columns(5)
            flag_vector(0)
            read_flag(0)
            for n in range(8, 12):
                split(n)
            for s in range(STEPS):
                if s == 0:
                    for t in range(TT):
                        gate_linear(1, t)
                if s == 4:
                    flag_vector(1)
                    read_flag(1)
                ffn_inner(s)
                if s == 0:
                    stats(3, 0)
                    stats(3, 1)
                if s == 1:
                    stats(3, 2)
                    stats(3, 3)
                if s == 2:
                    normalise(3)
                if s == 3:
                    guard_gate(1, bank[3])
                if 6 <= s < 10:
                    split(6 + s)
                if s == C + LAG - 1:
                    for t in range(TT):
                        gate_ffn(0, t)
            for t in range(TT):
                n = TT + t
                gate_ffn(1, t)
                if n >= BY_POOL:
                    dve.wait_ge(acc_read, n + 1)
                    dve.tensor_tensor(xt[:, n, :], xt[:, n, :], xn[:, t, :], ALU.add)\
                       .then_inc(out_last, 1)

        @block.tensor
        def _(pe):
            def mod_rows(n, w, src, dst):
                if n == 0:
                    pe.wait_ge(silu_c, 1)
                for j in range(KT):
                    last = pe.matmul(dst[32 * j:32 * (j + 1), 0:w], sc[:, j, :], src(j), start=True, stop=True)
                last.then_inc(rows_done, 1)

            def rows_ln1(k):
                pe.wait_ge(d_ln1[k], 16)
                if k:
                    pe.wait_ge(rows_copied, k)
                m = modw[:, k // 2, 2 * (k % 2):2 * (k % 2) + 2, :].rearrange("p a n -> p (a n)")
                mod_rows(k, D // 2, lambda j: m[:, j * (D // 2):(j + 1) * (D // 2)], bank[6])

            def columns(slot, count, dst):
                for i in range(count):
                    last = pe.transpose(dst[:, i * P:(i + 1) * P],
                                        rows[:, slot, i * P:(i + 1) * P], ident[:, :])
                last.then_inc(cols_done, 1)

            def columns_ln1(k):
                pe.wait_ge(rows_copied, k + 1)
                pe.wait_ge(keep_ok, k + 1)
                columns(k % 2, 2, bank[7])

            def mask_blocks(k):
                pe.wait_ge(msum_ok, k + 1)
                pe.wait_ge(consts_ok, 6)
                if k:
                    pe.wait_ge(modc_ok, k)
                pe.matmul(bank[7][:, 0:NBLK], blkones[:, :], msum[:, k, :], start=True, stop=True)\
                  .then_inc(blk_done, 1)

            def transposes(n):
                q, k = divmod(n, KT)
                dst = bank[4 + n % 2] if q < 2 else bank[n % 2] if q == 2 else bank[3]
                if k == 0:
                    pe.wait_ge(xn_ok, TT * (q + 1))
                if q == 2 and k < 2:
                    pe.wait_ge(att_read, k + 1)
                elif q == 3:
                    pe.wait_ge(h_ok, n)
                elif n >= 2:
                    pe.wait_ge(h_ok, n - 1)
                for t in range(TT):
                    last = pe.transpose(dst[:, t * P:(t + 1) * P], xn[:, t, k * P:(k + 1) * P],
                                        ident[:, :])
                last.then_inc(xt_done, 1)

            def linear(b, k, t):
                if t == 0:
                    pe.wait_ge(h_ok, TT * b + k + 1)
                    if b == 0:
                        pe.wait_ge(masked, k + 1)
                if b == 1 and k == 0:
                    if t < 2:
                        pe.wait_ge(h_ok, 7 + t)
                    else:
                        pe.wait_ge(gate_ok, t - 1)
                last = pe.matmul(bank[4 * b + t][:, :], h1[:, b, k, t * P:(t + 1) * P],
                                 awork[:, k, :], start=(k == 0), stop=(k == KT - 1))
                if k == KT - 1:
                    last.then_inc(att_done, 1)

            def gate_all(layer, b, dst):
                for k in range(KT):
                    last = pe.transpose(dst[:, k * P:(k + 1) * P],
                                        gcol[:, layer, k, b:b + 1].to_broadcast([P, P]),
                                        ident[:, :])
                last.then_inc(gate_done, 1)

            def flag_sum(g):
                pe.wait_ge(flagv_ok, g + 1)
                pe.matmul(bank[3][0:1, 0:1], flagv[:, g:g + 1], onecol[:, :], start=True, stop=True)\
                  .then_inc(flag_done, 1)

            general = []

            def load_flag(g):
                pe.wait_ge(flag_ok, g + 1)
                general.append(pe.value_load(flags[0:1, g:g + 1], min_val=0, max_val=1))

            def gate_up_product(s, u, k, part, native):
                b, c = divmod(s, C)
                w = whi_gu[:, s % 2, (u * KT + k) * P:(u * KT + k + 1) * P]
                h = ht[:, b, k, part, :]
                if native:
                    w, h = raw_gu(c, u, k), h.bitcast(F32)
                return pe.matmul(bank[gu_bank(s, u)][:, :], w, h, start=(k == 0 and part == 0),
                                 stop=(k == KT - 1 and part == 1))

            def gate_up_first():
                pe.wait_ge(wgu_hi, 1)
                pe.wait_ge(modc_ok, KT + 2)
                pe.wait_ge(h_ok, 11)

                def products(native):
                    for k in range(KT):
                        for part in range(2):
                            pe.wait_ge(h_lo if part else h_hi, k + 1)
                            for u in range(2):
                                last = gate_up_product(0, u, k, part, native)
                                if k == KT - 1 and part == 1:
                                    last.then_inc(up_mm if u else gate_mm, 1)

                with pe.If(general[0]):
                    products(True)
                with pe.Else():
                    products(False)

            def gate_up(s):
                b, c = divmod(s, C)
                pe.wait_ge(wgu_hi, s + 1)

                def products(native):
                    for u, done in ((0, gate_mm), (1, up_mm)):
                        if u == 1 and s > 1:
                            pe.wait_ge(silu_ok, s)
                        for k in range(KT):
                            if c == 0 and u == 0:
                                pe.wait_ge(h_lo, TT * b + k + 1)
                            for part in range(2):
                                last = gate_up_product(s, u, k, part, native)
                        last.then_inc(done, 1)

                if s == 1:
                    pe.wait_ge(h_ok, 12)
                else:
                    pe.wait_ge(inner_ok, s - 1)
                with pe.If(general[GROUP_OF[c]]):
                    products(True)
                with pe.Else():
                    products(False)

            def down_product(s, t, native):
                b, c = divmod(s, C)
                for part in range(2):
                    h = in_split[:, s % 3, part, t * P:(t + 1) * P]
                    w = whi_d(s)
                    if native:
                        h, w = h.bitcast(F32), raw_d(c)
                    last = pe.matmul(bank[4 + t][:, :], h, w, start=(c == 0 and part == 0),
                                     stop=(c == C - 1 and part == 1))
                if c == C - 1:
                    last.then_inc(acc_mm, 1)
                elif t == TT - 1:
                    last.then_inc(down_mm, 1)

            def down(s):
                b, c = divmod(s, C)
                pe.wait_ge(in_lo, s + 1)
                pe.wait_ge(wd_hi, s + 1)
                if c == 0:
                    if b == 0:
                        pe.wait_ge(att_read, 2 * TT)
                    else:
                        pe.wait_ge(acc_read, TT)
                with pe.If(general[GROUP_OF[c]]):
                    for t in range(TT):
                        down_product(s, t, True)
                with pe.Else():
                    for t in range(TT):
                        down_product(s, t, False)

            def down_last():
                o, a, z = STEPS - 3, STEPS - 2, STEPS - 1
                pe.wait_ge(in_lo, a + 1)
                pe.wait_ge(wd_hi, a + 1)

                def products(native):
                    for i, (s, t) in enumerate([(o, 0), (a, 0), (o, 1), (a, 1), (o, 2), (z, 0),
                                                (z, 1), (a, 2), (z, 2), (o, 3), (a, 3), (z, 3)]):
                        if i == 5:
                            pe.wait_ge(in_lo, z + 1)
                            pe.wait_ge(wd_hi, z + 1)
                        down_product(s, t, native)

                with pe.If(general[-1]):
                    products(True)
                with pe.Else():
                    products(False)

            def gate_rows():
                pe.wait_ge(d_gate[0], 16)
                pe.wait_ge(rows_copied, KT)
                mod_rows(4, D, lambda j: modw[:, 2, j, :], bank[6])

            def gate_columns():
                pe.wait_ge(rows_copied, KT + 1)
                pe.wait_ge(modc_ok, KT)
                columns(2, KT, bank[7])

            def gate_first(b):
                pe.wait_ge(gate_m, 1)
                gate_all(0, b, bank[6 + b])

            pe.wait_ge(ident_ok, 1)
            for _ in range(WARM_UP):
                pe.matmul(bank[0][:, 0:P], ident[:, :], ident[:, :], start=True, stop=True)
            rows_ln1(0)
            mask_blocks(0)
            columns_ln1(0)
            transposes(0)
            transposes(1)
            mask_blocks(1)
            rows_ln1(1)
            between = {
                (0, 0): [lambda: columns_ln1(1)],
                (0, 2): [lambda: mask_blocks(2), lambda: transposes(2)],
                (0, 3): [lambda: rows_ln1(2)],
                (1, 0): [lambda: columns_ln1(2)],
                (1, 1): [lambda: mask_blocks(3), lambda: rows_ln1(3)],
                (1, 2): [lambda: transposes(3)],
                (1, 3): [lambda: columns_ln1(3)],
                (2, 3): [gate_rows],
                (3, 0): [lambda: transposes(4), gate_columns],
                (3, 1): [lambda: transposes(5)],
                (3, 2): [lambda: gate_first(0), lambda: transposes(6)],
                (3, 3): [lambda: transposes(7), lambda: gate_first(1)],
            }
            for k in range(KT):
                for t in range(TT):
                    linear(0, k, t)
                    for more in between.get((k, t), []):
                        more()
            for k in range(KT):
                for t in range(TT):
                    linear(1, k, t)
                    if (k, t) == (0, 3):
                        pe.wait_ge(d_ln2[0], 16)
                        pe.wait_ge(att_read, 3)
                        mod_rows(5, D, lambda j: modw[:, 0, j, :], bank[2])
                    if (k, t) == (1, 1):
                        pe.wait_ge(rows_copied, 6)
                        pe.wait_ge(att_read, 4)
                        columns(0, KT, bank[3])
                        pe.wait_ge(d_ln2[1], 16)
                        mod_rows(6, D, lambda j: modw[:, 1, j, :], bank[2])
                    if (k, t) == (1, 3):
                        pe.wait_ge(rows_copied, 7)
                        columns(1, KT, bank[2])
                    if (k, t) == (2, 2):
                        transposes(8)
                        transposes(9)
                    if (k, t) == (2, 3):
                        pe.wait_ge(modc_ok, KT + 1)
                        flag_sum(0)
                    if (k, t) == (3, 0):
                        transposes(10)
                    if (k, t) == (3, 1):
                        transposes(11)
                        load_flag(0)
            for s in range(STEPS):
                if s == GROUPS[1][0]:
                    load_flag(1)
                if s == 0:
                    gate_up_first()
                else:
                    gate_up(s)
                if s == 4:
                    pe.wait_ge(cols_ok, 8)
                    flag_sum(1)
                if LAG <= s < STEPS - 1:
                    down(s - LAG)
                if s == 2:
                    pe.wait_ge(d_gate[1], 16)
                    pe.wait_ge(inner_ok, 2)
                    mod_rows(7, D, lambda j: modw[:, 2, j, :], bank[3])
                if s == 3:
                    pe.wait_ge(rows_copied, 8)
                    columns(2, KT, bank[3])
                if 6 <= s < 10:
                    transposes(6 + s)
                if s == 10:
                    pe.wait_ge(h_ok, 4 * TT)
                    gate_all(1, 0, bank[3])
                if s == 11:
                    pe.wait_ge(gate_ok, 3)
                    gate_all(1, 1, bank[3])
            down_last()


def kernel(L0_attn_data, L0_attn_weight, L0_attn_mask, L0_ffn_Wg, L0_ffn_Wu, L0_ffn_Wd, L0_ffn_ag,
           L0_ffn_au, L0_ffn_ad, L0_c, L0_wmod):
    import numpy as np
    from concourse import bacc
    from concourse.bass_utils import run_bass_kernel_spmd

    def c_(a):
        return np.ascontiguousarray(a)

    x = np.asarray(L0_attn_data)
    shape = x.shape
    nf = C - 1
    wmod = np.asarray(L0_wmod).reshape(KT, P, 6, D)

    def ln_weights(scale, shift):
        w = wmod[:, :, [scale, shift], :].reshape(KT, P, 2, KT, P)
        return w.transpose(3, 1, 0, 2, 4)

    gu = np.stack([np.asarray(L0_ffn_Wg), np.asarray(L0_ffn_Wu)])
    gu_full = gu[:, :nf * P].reshape(2, nf, P, KT, P).transpose(1, 4, 0, 3, 2)
    gu_tail = gu[:, nf * P:].reshape(2, FT, KT, P).transpose(3, 0, 2, 1)
    sc = np.stack([np.asarray(L0_ffn_ag), np.asarray(L0_ffn_au)])
    ln2 = ln_weights(4, 3).reshape(2, 2, P, KT, 2 * P).transpose(0, 2, 3, 1, 4)
    arrays = {
        "x": c_(x.reshape(NB * SEQ, D)),
        "att_w": c_(np.asarray(L0_attn_weight).T),
        "att_mask": c_(np.asarray(L0_attn_mask).T),
        "cond": c_(np.asarray(L0_c).T.reshape(KT, P, NB).transpose(1, 0, 2)),
        "mod_ln1": c_(ln_weights(1, 0).reshape(KT, P, 2, D)),
        "mod_ln2": c_(ln2.reshape(2, P, KT, D)),
        "mod_gate": c_(wmod[:, :, [2, 5], :].transpose(2, 1, 0, 3)),
        "w_gu": c_(gu_full.reshape(nf, P, 2 * D)),
        "w_gu_tail": c_(gu_tail.reshape(P, 2 * KT, FT)),
        "w_down": c_(np.asarray(L0_ffn_Wd).T),
        "scales": c_(sc[:, :nf * P].reshape(2, nf, P).transpose(2, 1, 0)),
        "scales_tail": c_(sc[:, nf * P:].T),
        "down_scale": c_(np.asarray(L0_ffn_ad).reshape(KT, P).T),
    }
    nc = bacc.Bacc("TRN2", target_bir_lowering=False, num_devices=1)
    args = [nc.dram_tensor(f"in_{name}", a.shape, mybir.dt.from_np(a.dtype), kind="ExternalInput").ap()
            for name, a in arrays.items()]
    args.append(nc.dram_tensor("out_0", (NB * SEQ, D), F32, kind="ExternalOutput").ap())
    adaln_block(nc, *args)
    r = run_bass_kernel_spmd(nc, [{f"in_{name}": a for name, a in arrays.items()}], core_ids=[0])
    return r.results[0]["out_0"].reshape(shape)
```
